# Optimizing a Trainium2 kernel written in Bass

```python
import numpy as np
import jax
import jax.numpy as jnp

def _softmax(x, axis=-1):
    return jax.nn.softmax(x, axis=axis)

def _gelu(x):
    return jax.nn.gelu(x, approximate=True)

def _silu(x):
    return jax.nn.silu(x)

def _sigmoid(x):
    return jax.nn.sigmoid(x)

def _layernorm(x, axis=-1, eps=1e-05):
    m = jnp.mean(x, axis=axis, keepdims=True)
    v = jnp.var(x, axis=axis, keepdims=True)
    return (x - m) / jnp.sqrt(v + eps)

def _scatter_add(tgt, idx, src, axis=0):
    return tgt.at[idx].add(src)

def _segment_sum(src, seg, n):
    return jax.ops.segment_sum(src, seg, n)
kernel_name = 'mk_vit_tower_postln_d2_tok_img768_r4_07f5bb'

def setup_inputs(seed: int=0):
    np.random.seed(seed)
    _w = jnp.asarray

    def _rec_inputs():
        import jax
        import jax.numpy as jnp
        _rk = jax.random.key(seed)
        x = -0.000348323 + 0.999952 * jax.random.normal(jax.random.fold_in(_rk, 1), (64, 3, 64, 64), jnp.float32)
        return x
    x = _rec_inputs()

    def _L0_tok_setup():
        import jax, jax.numpy as jnp
        import numpy as np
        PATCH = 16
        DIM = 192
        LN_EPS = 1e-05

        def _spt_forward(x, ln_gamma, ln_beta, w, b):
            B, C, H, W = x.shape
            p = PATCH
            x_right = jnp.pad(x, ((0, 0), (0, 0), (0, 0), (1, 0)))[:, :, :, :-1]
            x_left = jnp.pad(x, ((0, 0), (0, 0), (0, 0), (0, 1)))[:, :, :, 1:]
            x_down = jnp.pad(x, ((0, 0), (0, 0), (1, 0), (0, 0)))[:, :, :-1, :]
            x_up = jnp.pad(x, ((0, 0), (0, 0), (0, 1), (0, 0)))[:, :, 1:, :]
            xc = jnp.concatenate((x, x_right, x_left, x_down, x_up), axis=1)
            C5 = 5 * C
            h, wgrid = (H // p, W // p)
            tokens = xc.reshape(B, C5, h, p, wgrid, p)
            tokens = tokens.transpose(0, 2, 4, 3, 5, 1)
            tokens = tokens.reshape(B, h * wgrid, p * p * C5)
            mean = jnp.mean(tokens, axis=-1, keepdims=True)
            var = jnp.var(tokens, axis=-1, keepdims=True)
            normed = (tokens - mean) * jax.lax.rsqrt(var + LN_EPS) * ln_gamma + ln_beta
            return jnp.einsum('bnd,de->bne', normed, w) + b
        key = jax.random.key(seed)
        k1, k2 = jax.random.split(key)
        B, C, H, W = (32, 3, 96, 96)
        patch_dim = PATCH * PATCH * 5 * C
        x = jax.random.normal(k1, (B, C, H, W), dtype=jnp.float32)
        ln_gamma = jnp.ones((patch_dim,), dtype=jnp.float32)
        ln_beta = jnp.zeros((patch_dim,), dtype=jnp.float32)
        w = jax.random.normal(k2, (patch_dim, DIM), dtype=jnp.float32) * patch_dim ** (-0.5)
        b = jnp.zeros((DIM,), dtype=jnp.float32)
        return {'x': x, 'ln_gamma': ln_gamma, 'ln_beta': ln_beta, 'w': w, 'b': b}
    _L0_tok_all = _L0_tok_setup()
    _L0_tok_in = {k: v for k, v in _L0_tok_all.items() if k in ('ln_gamma', 'ln_beta', 'w', 'b')}
    del _L0_tok_all

    def _L0_attn_setup():
        import jax, jax.numpy as jnp
        import numpy as np
        DIM = 192
        HEADS = 12
        HEAD_DIM = DIM // HEADS
        EPS = 1e-12

        def _l1_normalize(t):
            denom = jnp.maximum(jnp.sum(jnp.abs(t), axis=-2, keepdims=True), EPS)
            return t / denom
        key = jax.random.key(seed)
        k1, k2, k3 = jax.random.split(key, 3)
        x = jax.random.normal(k1, (8, 1024, DIM), dtype=jnp.float32)
        s = 1.0 / np.sqrt(DIM)
        w_qkv = jax.random.uniform(k2, (3 * DIM, DIM), dtype=jnp.float32, minval=-s, maxval=s)
        w_proj = jax.random.uniform(k3, (DIM, DIM), dtype=jnp.float32, minval=-s, maxval=s)
        b_proj = jnp.zeros((DIM,), dtype=jnp.float32)
        return {'x': x, 'w_qkv': w_qkv, 'w_proj': w_proj, 'b_proj': b_proj}
    _L0_attn_all = _L0_attn_setup()
    _L0_attn_in = {k: v for k, v in _L0_attn_all.items() if k in ('w_qkv', 'w_proj', 'b_proj')}
    del _L0_attn_all

    def _L0_ffn_setup():
        import jax, jax.numpy as jnp
        import numpy as np
        DIM = 192
        HEADS = 12
        HIDDEN = 768
        E = 8
        TOPK = 2
        EPS = 1e-05

        def _ln(x, g, b):
            m = x.mean(-1, keepdims=True)
            v = jnp.mean((x - m) ** 2, axis=-1, keepdims=True)
            return (x - m) * jax.lax.rsqrt(v + EPS) * g + b
        key = jax.random.key(seed)
        ks = jax.random.split(key, 10)
        s = 0.02
        return {'x': jax.random.normal(ks[0], (8, 256, DIM), jnp.float32), 'ln1_g': jnp.ones((DIM,), jnp.float32), 'ln1_b': jnp.zeros((DIM,), jnp.float32), 'qkv_w': jax.random.normal(ks[1], (DIM, 3 * DIM), jnp.float32) * s, 'proj_w': jax.random.normal(ks[2], (DIM, DIM), jnp.float32) * s, 'proj_b': jnp.zeros((DIM,), jnp.float32), 'ln2_g': jnp.ones((DIM,), jnp.float32), 'ln2_b': jnp.zeros((DIM,), jnp.float32), 'gate_w': jax.random.normal(ks[3], (DIM, E), jnp.float32) * s, 'gate_b': jnp.zeros((E,), jnp.float32), 'w1': jax.random.normal(ks[4], (E, DIM, HIDDEN), jnp.float32) * s, 'b1': jnp.zeros((E, HIDDEN), jnp.float32), 'w2': jax.random.normal(ks[5], (E, HIDDEN, DIM), jnp.float32) * s, 'b2': jnp.zeros((E, DIM), jnp.float32)}
    _L0_ffn_all = _L0_ffn_setup()
    _L0_ffn_in = {k: v for k, v in _L0_ffn_all.items() if k in ('ln1_g', 'ln1_b', 'qkv_w', 'proj_w', 'proj_b', 'ln2_g', 'ln2_b', 'gate_w', 'gate_b', 'w1', 'b1', 'w2', 'b2')}
    del _L0_ffn_all

    def _L1_attn_setup():
        import jax, jax.numpy as jnp
        import numpy as np
        D_MODEL = 192
        D_STATE = 16
        D_CONV = 4
        EXPAND = 2
        D_INNER = EXPAND * D_MODEL
        BATCH = 2
        SEQLEN = 1024

        def _silu(x):
            return x * jax.nn.sigmoid(x)
        key = jax.random.key(seed)
        ks = jax.random.split(key, 8)
        s = 0.02
        return {'hidden_states': jax.random.normal(ks[0], (BATCH, SEQLEN, D_MODEL), jnp.float32), 'W_in': jax.random.normal(ks[1], (D_MODEL, 2 * D_INNER), jnp.float32) * s, 'conv_w': jax.random.normal(ks[2], (D_INNER, 1, D_CONV), jnp.float32) * s, 'conv_b': jnp.zeros((D_INNER,), jnp.float32), 'W_x': jax.random.normal(ks[3], (D_INNER, 2 * D_STATE + D_INNER), jnp.float32) * s, 'W_dt': jax.random.normal(ks[4], (D_INNER, D_INNER), jnp.float32) * s, 'b_dt': jnp.zeros((D_INNER,), jnp.float32), 'A_log': jax.random.uniform(ks[5], (D_INNER, D_STATE), jnp.float32, minval=-1.0, maxval=0.0), 'D': jnp.ones((D_INNER,), jnp.float32), 'W_out': jax.random.normal(ks[6], (D_INNER, D_MODEL), jnp.float32) * s}
    _L1_attn_all = _L1_attn_setup()
    _L1_attn_in = {k: v for k, v in _L1_attn_all.items() if k in ('W_in', 'conv_w', 'conv_b', 'W_x', 'W_dt', 'b_dt', 'A_log', 'D', 'W_out')}
    del _L1_attn_all

    def _L1_ffn_setup():
        import jax, jax.numpy as jnp
        import numpy as np
        from jax import lax
        DIM = 192
        INTER = 128
        E = 8
        G = 4
        TOPK_G = 2
        TOPK = 2
        ROUTE_SCALE = 1.0

        def _gate(x2, gate_weight, gate_bias):
            T = x2.shape[0]
            scores = jax.nn.sigmoid(x2 @ gate_weight.T)
            s = scores + gate_bias
            sv = s.reshape(T, G, E // G)
            top2, _ = lax.top_k(sv, 2)
            group_scores = top2.sum(-1)
            _, gidx = lax.top_k(group_scores, TOPK_G)
            gmask = jnp.zeros((T, G), bool).at[jnp.arange(T)[:, None], gidx].set(True)
            masked = jnp.where(gmask[:, :, None], sv, -jnp.inf).reshape(T, E)
            _, idx = lax.top_k(masked, TOPK)
            w = jnp.take_along_axis(scores, idx, axis=1)
            w = w / (w.sum(-1, keepdims=True) + 1e-06) * ROUTE_SCALE
            return (w, idx)
        key = jax.random.key(seed)
        ks = jax.random.split(key, 9)
        s = 1.0 / np.sqrt(DIM)
        si = 1.0 / np.sqrt(INTER)
        return {'x': jax.random.normal(ks[0], (4, 1024, DIM), jnp.float32), 'gate_weight': jax.random.uniform(ks[1], (E, DIM), jnp.float32, -s, s), 'gate_bias': jnp.zeros((E,), jnp.float32), 'w1': jax.random.uniform(ks[2], (E, INTER, DIM), jnp.float32, -s, s), 'w2': jax.random.uniform(ks[3], (E, DIM, INTER), jnp.float32, -si, si), 'w3': jax.random.uniform(ks[4], (E, INTER, DIM), jnp.float32, -s, s), 'sw1': jax.random.uniform(ks[5], (INTER, DIM), jnp.float32, -s, s), 'sw2': jax.random.uniform(ks[6], (DIM, INTER), jnp.float32, -si, si), 'sw3': jax.random.uniform(ks[7], (INTER, DIM), jnp.float32, -s, s)}
    _L1_ffn_all = _L1_ffn_setup()
    _L1_ffn_in = {k: v for k, v in _L1_ffn_all.items() if k in ('gate_weight', 'gate_bias', 'w1', 'w2', 'w3', 'sw1', 'sw2', 'sw3')}
    del _L1_ffn_all
    return {'x': x, 'L0_tok_ln_gamma': _L0_tok_in['ln_gamma'], 'L0_tok_ln_beta': _L0_tok_in['ln_beta'], 'L0_tok_w': _L0_tok_in['w'], 'L0_tok_b': _L0_tok_in['b'], 'L0_attn_w_qkv': _L0_attn_in['w_qkv'], 'L0_attn_w_proj': _L0_attn_in['w_proj'], 'L0_attn_b_proj': _L0_attn_in['b_proj'], 'L0_ffn_ln1_g': _L0_ffn_in['ln1_g'], 'L0_ffn_ln1_b': _L0_ffn_in['ln1_b'], 'L0_ffn_qkv_w': _L0_ffn_in['qkv_w'], 'L0_ffn_proj_w': _L0_ffn_in['proj_w'], 'L0_ffn_proj_b': _L0_ffn_in['proj_b'], 'L0_ffn_ln2_g': _L0_ffn_in['ln2_g'], 'L0_ffn_ln2_b': _L0_ffn_in['ln2_b'], 'L0_ffn_gate_w': _L0_ffn_in['gate_w'], 'L0_ffn_gate_b': _L0_ffn_in['gate_b'], 'L0_ffn_w1': _L0_ffn_in['w1'], 'L0_ffn_b1': _L0_ffn_in['b1'], 'L0_ffn_w2': _L0_ffn_in['w2'], 'L0_ffn_b2': _L0_ffn_in['b2'], 'L1_attn_W_in': _L1_attn_in['W_in'], 'L1_attn_conv_w': _L1_attn_in['conv_w'], 'L1_attn_conv_b': _L1_attn_in['conv_b'], 'L1_attn_W_x': _L1_attn_in['W_x'], 'L1_attn_W_dt': _L1_attn_in['W_dt'], 'L1_attn_b_dt': _L1_attn_in['b_dt'], 'L1_attn_A_log': _L1_attn_in['A_log'], 'L1_attn_D': _L1_attn_in['D'], 'L1_attn_W_out': _L1_attn_in['W_out'], 'L1_ffn_gate_weight': _L1_ffn_in['gate_weight'], 'L1_ffn_gate_bias': _L1_ffn_in['gate_bias'], 'L1_ffn_w1': _L1_ffn_in['w1'], 'L1_ffn_w2': _L1_ffn_in['w2'], 'L1_ffn_w3': _L1_ffn_in['w3'], 'L1_ffn_sw1': _L1_ffn_in['sw1'], 'L1_ffn_sw2': _L1_ffn_in['sw2'], 'L1_ffn_sw3': _L1_ffn_in['sw3']}

def reference(x, L0_tok_ln_gamma, L0_tok_ln_beta, L0_tok_w, L0_tok_b, L0_attn_w_qkv, L0_attn_w_proj, L0_attn_b_proj, L0_ffn_ln1_g, L0_ffn_ln1_b, L0_ffn_qkv_w, L0_ffn_proj_w, L0_ffn_proj_b, L0_ffn_ln2_g, L0_ffn_ln2_b, L0_ffn_gate_w, L0_ffn_gate_b, L0_ffn_w1, L0_ffn_b1, L0_ffn_w2, L0_ffn_b2, L1_attn_W_in, L1_attn_conv_w, L1_attn_conv_b, L1_attn_W_x, L1_attn_W_dt, L1_attn_b_dt, L1_attn_A_log, L1_attn_D, L1_attn_W_out, L1_ffn_gate_weight, L1_ffn_gate_bias, L1_ffn_w1, L1_ffn_w2, L1_ffn_w3, L1_ffn_sw1, L1_ffn_sw2, L1_ffn_sw3):
    import jax
    import jax.numpy as jnp

    def _L0_tok_ref(x, ln_gamma, ln_beta, w, b):
        import jax, jax.numpy as jnp
        import numpy as np
        PATCH = 16
        DIM = 192
        LN_EPS = 1e-05

        def _spt_forward(x, ln_gamma, ln_beta, w, b):
            B, C, H, W = x.shape
            p = PATCH
            x_right = jnp.pad(x, ((0, 0), (0, 0), (0, 0), (1, 0)))[:, :, :, :-1]
            x_left = jnp.pad(x, ((0, 0), (0, 0), (0, 0), (0, 1)))[:, :, :, 1:]
            x_down = jnp.pad(x, ((0, 0), (0, 0), (1, 0), (0, 0)))[:, :, :-1, :]
            x_up = jnp.pad(x, ((0, 0), (0, 0), (0, 1), (0, 0)))[:, :, 1:, :]
            xc = jnp.concatenate((x, x_right, x_left, x_down, x_up), axis=1)
            C5 = 5 * C
            h, wgrid = (H // p, W // p)
            tokens = xc.reshape(B, C5, h, p, wgrid, p)
            tokens = tokens.transpose(0, 2, 4, 3, 5, 1)
            tokens = tokens.reshape(B, h * wgrid, p * p * C5)
            mean = jnp.mean(tokens, axis=-1, keepdims=True)
            var = jnp.var(tokens, axis=-1, keepdims=True)
            normed = (tokens - mean) * jax.lax.rsqrt(var + LN_EPS) * ln_gamma + ln_beta
            return jnp.einsum('bnd,de->bne', normed, w) + b
        return _spt_forward(x, ln_gamma, ln_beta, w, b)

    def _L0_attn_ref(x, w_qkv, w_proj, b_proj):
        import jax, jax.numpy as jnp
        import numpy as np
        DIM = 192
        HEADS = 12
        HEAD_DIM = DIM // HEADS
        EPS = 1e-12

        def _l1_normalize(t):
            denom = jnp.maximum(jnp.sum(jnp.abs(t), axis=-2, keepdims=True), EPS)
            return t / denom
        B, N, C = x.shape
        hd = C // HEADS
        qkv = x @ w_qkv.T
        qkv = qkv.reshape(B, N, 3, HEADS, hd).transpose(2, 0, 3, 1, 4)
        q, k, v = (qkv[0], qkv[1], qkv[2])
        q = _l1_normalize(q)
        k = _l1_normalize(k)
        if N < hd:
            out = jnp.einsum('bhnd,bhmd,bhme->bhne', q, k, v)
        else:
            kv = jnp.einsum('bhnd,bhne->bhde', k, v)
            out = jnp.einsum('bhnd,bhde->bhne', q, kv)
        out = out.transpose(0, 2, 1, 3).reshape(B, N, C)
        return out @ w_proj.T + b_proj

    def _L0_ffn_ref(x, ln1_g, ln1_b, qkv_w, proj_w, proj_b, ln2_g, ln2_b, gate_w, gate_b, w1, b1, w2, b2):
        import jax, jax.numpy as jnp
        import numpy as np
        DIM = 192
        HEADS = 12
        HIDDEN = 768
        E = 8
        TOPK = 2
        EPS = 1e-05

        def _ln(x, g, b):
            m = x.mean(-1, keepdims=True)
            v = jnp.mean((x - m) ** 2, axis=-1, keepdims=True)
            return (x - m) * jax.lax.rsqrt(v + EPS) * g + b
        B, S, D = x.shape
        hd = D // HEADS
        h = _ln(x, ln1_g, ln1_b)
        qkv = (h @ qkv_w).reshape(B, S, 3, HEADS, hd).transpose(2, 0, 3, 1, 4)
        q, k, v = (qkv[0], qkv[1], qkv[2])
        att = jax.nn.softmax(jnp.einsum('bhqd,bhkd->bhqk', q, k) * hd ** (-0.5), axis=-1)
        o = jnp.einsum('bhqk,bhkd->bhqd', att, v).transpose(0, 2, 1, 3).reshape(B, S, D)
        x = x + o @ proj_w + proj_b
        h2 = _ln(x, ln2_g, ln2_b).reshape(B * S, D)
        logits = h2 @ gate_w + gate_b
        wts, sel = jax.lax.top_k(logits, TOPK)
        wts = jax.nn.softmax(wts.astype(jnp.float32), axis=-1).astype(x.dtype)
        cw = (jax.nn.one_hot(sel, E, dtype=x.dtype) * wts[..., None]).sum(axis=1)
        res = jnp.zeros_like(h2)
        for e in range(E):
            he = jax.nn.gelu(h2 @ w1[e] + b1[e], approximate=False)
            res = res + cw[:, e:e + 1] * (he @ w2[e] + b2[e])
        return x + res.reshape(B, S, D)

    def _L1_attn_ref(hidden_states, W_in, conv_w, conv_b, W_x, W_dt, b_dt, A_log, D, W_out):
        import jax, jax.numpy as jnp
        import numpy as np
        D_MODEL = 192
        D_STATE = 16
        D_CONV = 4
        EXPAND = 2
        D_INNER = EXPAND * D_MODEL
        BATCH = 2
        SEQLEN = 1024

        def _silu(x):
            return x * jax.nn.sigmoid(x)
        B, L, _ = hidden_states.shape
        xz = hidden_states @ W_in
        x, z = (xz[..., :D_INNER], xz[..., D_INNER:])
        xc = jnp.swapaxes(x, 1, 2)
        xc = jax.lax.conv_general_dilated(xc, conv_w, window_strides=(1,), padding=[(D_CONV - 1, 0)], dimension_numbers=('NCH', 'OIH', 'NCH'), feature_group_count=D_INNER)
        x = jnp.swapaxes(xc, 1, 2) + conv_b
        x = _silu(x)
        xp = x @ W_x
        Bm = jax.nn.softmax(xp[..., :D_STATE], axis=-1)
        Cm = xp[..., D_STATE:2 * D_STATE]
        delta = jax.nn.softplus(xp[..., 2 * D_STATE:] @ W_dt + b_dt)
        A = -jnp.exp(A_log.astype(jnp.float32))

        def step(h, t):
            dt, Bt, Ct, ut = t
            dA = jnp.exp(dt[:, :, None] * A)
            h = dA * h + dt[:, :, None] * Bt[:, None, :] * ut[:, :, None]
            y = jnp.einsum('bs,bds->bd', Ct, h)
            return (h, y)
        h0 = jnp.zeros((B, D_INNER, D_STATE), x.dtype)
        ts = (jnp.swapaxes(delta, 0, 1), jnp.swapaxes(Bm, 0, 1), jnp.swapaxes(Cm, 0, 1), jnp.swapaxes(x, 0, 1))
        _, ys = jax.lax.scan(step, h0, ts)
        y = jnp.swapaxes(ys, 0, 1)
        y = y * _silu(z)
        return y @ W_out

    def _L1_ffn_ref(x, gate_weight, gate_bias, w1, w2, w3, sw1, sw2, sw3):
        import jax, jax.numpy as jnp
        import numpy as np
        from jax import lax
        DIM = 192
        INTER = 128
        E = 8
        G = 4
        TOPK_G = 2
        TOPK = 2
        ROUTE_SCALE = 1.0

        def _gate(x2, gate_weight, gate_bias):
            T = x2.shape[0]
            scores = jax.nn.sigmoid(x2 @ gate_weight.T)
            s = scores + gate_bias
            sv = s.reshape(T, G, E // G)
            top2, _ = lax.top_k(sv, 2)
            group_scores = top2.sum(-1)
            _, gidx = lax.top_k(group_scores, TOPK_G)
            gmask = jnp.zeros((T, G), bool).at[jnp.arange(T)[:, None], gidx].set(True)
            masked = jnp.where(gmask[:, :, None], sv, -jnp.inf).reshape(T, E)
            _, idx = lax.top_k(masked, TOPK)
            w = jnp.take_along_axis(scores, idx, axis=1)
            w = w / (w.sum(-1, keepdims=True) + 1e-06) * ROUTE_SCALE
            return (w, idx)
        B, S, D = x.shape
        x2 = x.reshape(-1, D)
        T = x2.shape[0]
        weights, indices = _gate(x2, gate_weight, gate_bias)
        cw = jnp.zeros((T, E), x.dtype).at[jnp.arange(T)[:, None], indices].add(weights)
        h1 = jnp.einsum('td,eid->tei', x2, w1)
        h3 = jnp.einsum('td,eid->tei', x2, w3)
        h = jax.nn.silu(h1) * h3
        y = jnp.einsum('tei,edi,te->td', h, w2, cw)
        z = jax.nn.silu(x2 @ sw1.T) * (x2 @ sw3.T) @ sw2.T
        return (y + z).reshape(B, S, D)
    h = _L0_tok_ref(x, L0_tok_ln_gamma, L0_tok_ln_beta, L0_tok_w, L0_tok_b)
    h = _layernorm(h + _L0_attn_ref(h, L0_attn_w_qkv, L0_attn_w_proj, L0_attn_b_proj), axis=-1)
    h = _layernorm(h + _L0_ffn_ref(h, L0_ffn_ln1_g, L0_ffn_ln1_b, L0_ffn_qkv_w, L0_ffn_proj_w, L0_ffn_proj_b, L0_ffn_ln2_g, L0_ffn_ln2_b, L0_ffn_gate_w, L0_ffn_gate_b, L0_ffn_w1, L0_ffn_b1, L0_ffn_w2, L0_ffn_b2), axis=-1)
    h = _layernorm(h + _L1_attn_ref(h, L1_attn_W_in, L1_attn_conv_w, L1_attn_conv_b, L1_attn_W_x, L1_attn_W_dt, L1_attn_b_dt, L1_attn_A_log, L1_attn_D, L1_attn_W_out), axis=-1)
    h = _layernorm(h + _L1_ffn_ref(h, L1_ffn_gate_weight, L1_ffn_gate_bias, L1_ffn_w1, L1_ffn_w2, L1_ffn_w3, L1_ffn_sw1, L1_ffn_sw2, L1_ffn_sw3), axis=-1)
    return h

_drawn_inputs = setup_inputs


def setup_inputs(seed=0):
    import zlib

    import numpy as np

    out = dict(_drawn_inputs(seed))
    spreads = {'L0_tok_ln_gamma': (1.0, 0.2),
     'L0_tok_ln_beta': (0.0, 0.1),
     'L0_tok_b': (0.0, 0.1),
     'L0_attn_b_proj': (0.0, 0.1),
     'L0_ffn_ln1_g': (1.0, 0.6),
     'L0_ffn_ln1_b': (0.0, 0.8),
     'L0_ffn_proj_b': (0.0, 0.1),
     'L0_ffn_ln2_g': (1.0, 0.6),
     'L0_ffn_ln2_b': (0.0, 0.588),
     'L0_ffn_gate_b': (0.0, 0.1),
     'L0_ffn_b1': (0.0, 0.669),
     'L0_ffn_b2': (0.0, 0.1),
     'L1_attn_conv_b': (0.0, 0.8),
     'L1_attn_b_dt': (0.0, 0.8),
     'L1_attn_D': (1.0, 0.2),
     'L1_ffn_gate_bias': (0.0, 0.1)}
    factors = {'L0_ffn_qkv_w': 3.448,
     'L0_ffn_proj_w': 3.676,
     'L1_attn_W_in': 8.0,
     'L1_attn_conv_w': 8.0,
     'L1_attn_W_x': 8.0,
     'L1_attn_W_dt': 8.0,
     'L1_attn_A_log': 8.0,
     'L1_attn_W_out': 8.0}
    for name, (base, spread) in spreads.items():
        noise = np.random.default_rng([zlib.crc32(name.encode()), seed]).standard_normal(out[name].shape)
        drawn = base * np.exp(spread * noise) if base else spread * noise
        out[name] = jnp.asarray(drawn.astype(out[name].dtype))
    for name, factor in factors.items():
        out[name] = (out[name] * factor).astype(out[name].dtype)
    return out
```

```python
import concourse.bass as bass
from concourse import mybir
from contextlib import ExitStack

F32 = mybir.dt.float32
BF16 = mybir.dt.bfloat16
ALU = mybir.AluOpType
ACT = mybir.ActivationFunctionType
AX = mybir.AxisListType

IMAGES, CHANNELS, SIDE, PATCH = 64, 3, 64, 16
SEQ = (SIDE // PATCH) ** 2
TOKENS = IMAGES * SEQ
DIM, HEADS = 192, 12
HD = DIM // HEADS
HALF = DIM // 2
HH = HEADS // 2
P = 128
BT = 256
U = BT // P
BLOCKS = TOKENS // BT
BI = BT // SEQ
PATCH_DIM = PATCH * PATCH * 5 * CHANNELS
SHIFTS = 5
PIXELS = CHANNELS * (PATCH * PATCH + 4 * PATCH)
PR = 120
PK = PIXELS // PR
EXPERTS, HIDDEN = 8, 768
HM = HIDDEN // P
INNER, STATE, TAPS = 384, 16, 4
CH = INNER // P
INTER = 128
FFN = EXPERTS + 1
EPS = 1e-5
FAR = 1e30

C_IDENT = 0
C_MASK = C_IDENT + P
C_NEG = C_MASK + 32
C_HEAD = C_NEG + 32
C_TRI = C_HEAD + HH
C_CNT = C_TRI + 64
C_END = C_CNT + PK

class Signal:

    def __init__(self, sem, per):
        self.sem, self.per = sem, per

    def at(self, i, k):
        return i * self.per + k

def first(i):
    return isinstance(i, int) and i == 0

class Chain:

    def __init__(self, eng, sig):
        self.eng, self.sig, self.i, self.n = eng, sig, 0, 0

    def start(self, i):
        self.i, self.n = i, 0

    def end(self):
        assert self.n == self.sig.per, (self.n, self.sig.per)

    def step(self, ins):
        self.n += 1
        ins.then_inc(self.sig.sem, 1)
        return self.n

    def after(self, n):
        self.eng.wait_ge(self.sig.sem, self.sig.at(self.i, n))

    def link(self, ins):
        self.after(self.step(ins))

def tower(nc, d, out):
    ctx = ExitStack()
    with ctx:
        def sb(name, shape, dt=F32):
            return ctx.enter_context(nc.sbuf_tensor(name, shape, dt))

        def bank(name):
            return ctx.enter_context(nc.psum_tensor(name, [P, 512], F32))

        def signal(name, per=1):
            return Signal(ctx.enter_context(nc.semaphore(name)), per)

        cst = sb("cst", [P, C_END])
        ident = cst[:, C_IDENT:C_IDENT + P]
        mask = cst[:, C_MASK:C_MASK + 32]
        neg = cst[:, C_NEG:C_NEG + 32]
        tri = cst[:, C_TRI:C_TRI + 64].rearrange("p (e f) -> p e f", e=8)
        cnt = cst[0:PR, C_CNT:C_CNT + PK]
        rows = sb("rows", [P, 3 * DIM + 16])
        tok_b, proj1_b, proj2_b = (rows[:, n * DIM:(n + 1) * DIM] for n in range(3))
        gate0_b, gate1_b = rows[:, 3 * DIM:3 * DIM + 8], rows[:, 3 * DIM + 8:3 * DIM + 16]
        ln12 = sb("ln12", [HALF, 8])
        tokgb = sb("tokgb", [PR, 2, SHIFTS, PK])
        qkv_w = [sb(f"qkv_w{n}", [HALF, 2, 3 * DIM]) for n in range(2)]
        proj_w = [sb(f"proj_w{n}", [HALF, 2, DIM]) for n in range(2)]
        gate0_w = sb("gate0_w", [HALF, 2, EXPERTS])
        w1 = [sb(f"w1_{n}", [HALF, 2, HIDDEN]) for n in range(2)]
        b1 = sb("b1", [P, EXPERTS * HM])
        w2 = [sb(f"w2_{n}", [P, HM, DIM]) for n in range(2)]
        b2 = sb("b2", [EXPERTS, DIM])
        in_w = sb("in_w", [HALF, 2, 2 * INNER])
        cols = sb("cols", [P, CH, TAPS + 2 + STATE])
        x_w = sb("x_w", [P, CH, 2 * STATE + INNER])
        dt_w = sb("dt_w", [P, CH, INNER])
        out_w = sb("out_w", [P, CH, DIM])
        gate1_w = sb("gate1_w", [HALF, 2, EXPERTS])
        f1_w = sb("f1_w", [HALF, 2, FFN * INTER])
        f3_w = sb("f3_w", [HALF, 2, FFN * INTER])
        f2_w = sb("f2_w", [INTER, FFN, DIM])

        tokw = sb("tokw", [PR, PK, DIM + 1])
        tok_cs = sb("tok_cs", [P, DIM])
        tok_bw = sb("tok_bw", [P, DIM])
        ones = sb("ones", [P, P])
        idle = sb("idle", [P, 1])
        half_neg = sb("half_neg", [P, U])
        identb = sb("identb", [P, P], BF16)
        pick = sb("pick", [HALF, 32], BF16)
        decay = sb("decay", [P, CH, STATE])

        xb = sb("xb", [PR, PK, BT])
        shared = sb("shared", [P, 2 * HM * BT])
        sq = shared[0:PR, 0:PK * BT].rearrange("p (k t) -> p k t", k=PK)
        kx = shared[0:HALF, :].rearrange("p (m h t) -> p m h t", m=2, h=HH)
        he = [shared[:, n * HM * BT:(n + 1) * HM * BT].rearrange("p (m t) -> p m t", m=HM) for n in range(2)]
        st = sb("st", [P, U, 6])
        mv = sb("mv", [P, U, 2])
        ve = sb("ve", [P, U])
        rstd = sb("rstd", [P, U])
        tmp = sb("tmp", [P, U, DIM])
        h0, hb, h1, z, xm, acc = (sb(n, [P, U, DIM]) for n in ("h0", "hb", "h1", "z", "xm", "acc"))
        hT = sb("hT", [HALF, 2, BT])
        qT = sb("qT", [HALF, 2, BT])
        kT = sb("kT", [HALF, 2, BT])
        vt = sb("vt", [P, U, DIM])
        l1 = sb("l1", [HALF, 2, 2 * BI])
        pm = sb("pm", [P, U, HEADS, 32])
        pbd = sb("pbd", [P, U * HEADS, P])
        mx = sb("mx", [P, U * HEADS])
        ot = sb("ot", [P, U, DIM])
        oT = sb("oT", [HALF, 2, BT])
        h2T = sb("h2T", [HALF, 2, BT])
        lg = sb("lg", [P, U, 8])
        rk = sb("rk", [P, U, 8, 8])
        req = sb("req", [P, U, 8, 8])
        rank = sb("rank", [P, U, 8])
        g1 = sb("g1", [P, U, 1])
        gd = sb("gd", [P, U, 8])
        ge = sb("ge", [P, U, 8])
        cw = sb("cw", [P, U, 8])
        cwT = sb("cwT", [EXPERTS, BT])

        h3 = sb("h3", [P, U, DIM])
        h3T = sb("h3T", [HALF, 2, BT])
        LONG = CH * BT
        RAW = SHIFTS * PK * DIM
        long = sb("long", [P, RAW])
        at = [0]

        def part(n):
            at[0] += n
            return long[:, at[0] - n:at[0]]

        uc, sz, uu, dtp, delta, yy = (part(LONG).rearrange("p (c t) -> p c t", c=CH) for _ in range(6))
        dab, du = uc, dtp
        SLOTS = 4
        hs = [part(2 * BT) for _ in range(SLOTS)]
        h4, rb = (part(U * DIM).rearrange("p (u e) -> p u e", u=U) for _ in range(2))
        wraw = long[0:PR, :].rearrange("p (s k e) -> p s k e", s=SHIFTS, k=PK)
        xpad = sb("xpad", [P, CH, BI, SEQ + TAPS - 1])
        bm = sb("bm", [P, U, 1])
        bd = sb("bd", [P, U, STATE])
        be = sb("be", [P, U, STATE])
        bcf = sb("bcf", [P, U, 2 * STATE])
        bres = sb("bres", [P, U, 2 * STATE])
        bc3 = sb("bc3", [P, U, 3, 2 * STATE], BF16)
        bcT = sb("bcT", [HALF, BT], BF16)
        dA = [sb(f"dA{n}", [P, 2 * BI, SEQ]) for n in range(3)]
        stb = sb("stb", [P, U, 6])
        mvb = sb("mvb", [P, U, 2])
        veb = sb("veb", [P, U])
        rstdb = sb("rstdb", [P, U])
        fin = sb("fin", [P, U, DIM])
        h4T = h3T
        th = sb("th", [P, U, 8])
        sc = sb("sc", [P, U, 8])
        sbias = sb("sbias", [P, U, 8])
        gs = sb("gs", [P, U, 4])
        gr = sb("gr", [P, U, 4])
        cw2 = sb("cw2", [P, U, 8])
        b_rk = sb("b_rk", [P, U, 8, 8])
        b_req = sb("b_req", [P, U, 8, 8])
        b_rank = sb("b_rank", [P, U, 8])
        b_g1 = sb("b_g1", [P, U, 1])
        sg = [sb(f"sg{n}", [P, BT]) for n in range(2)]
        gg = [sb(f"gg{n}", [P, BT]) for n in range(2)]

        A, B, C, D = (bank(f"front{n}") for n in range(4))
        Q = [bank(f"back{n}") for n in range(4)]

        loads = ["cst", "tok", "rows", "attn1", "attn2", "gate0", "scan", "ffn"]
        ld = {n: signal("loaded_" + n) for n in loads}
        x_loaded = signal("x_loaded", 16)
        w1_loaded = [signal(f"w1_loaded{n}", 16 * EXPERTS // 2) for n in range(2)]
        w2_loaded = [signal(f"w2_loaded{n}", 16 * EXPERTS // 2) for n in range(2)]
        ready = signal("constants_ready")
        beta_mm, tokw_ready, colsum_mm = signal("beta_mm"), signal("tokw_ready"), signal("colsum_mm")
        tok_mm = signal("tok_mm", 2)
        sq_ready = signal("sq_ready")
        var_f, rstd_f = signal("var_f", 5), signal("rstd_f", 5)
        h_f = signal("h_f", 3)
        t_f, tc_f = signal("t_f", 5), signal("tc_f", 5)
        h0b_ready, h1_ready, h1b_ready = signal("h0b_ready"), signal("h1_ready"), signal("h1b_ready")
        xm_ready, hx_ready = signal("xm_ready"), signal("hx_ready")
        qkv_mm = signal("qkv_mm", 2)
        q_ready = signal("q_ready", 2)
        k_ready = signal("k_ready", 2)
        kx_ready, v_ready = signal("kx_ready", 2), signal("v_ready", 2)
        s_mm = signal("s_mm", 2)
        sm_in, sm_out = signal("sm_in"), signal("sm_out")
        pbd_ready, pv_mm, o_ready = signal("pbd_ready", 2), signal("pv_mm", 2), signal("o_ready", 2)
        proj_mm = signal("proj_mm", 2)
        gate_mm, gate_in, gate_out = signal("gate_mm"), signal("gate_in"), signal("gate_out")
        cw_ready, cwT_mm, cwT_ready, b2_mm = (signal("cw_ready"), signal("cwT_mm"), signal("cwT_ready"),
                                              signal("b2_mm"))
        acc0_ready = signal("acc0_ready")
        hid_mm, hid_ready = signal("hid_mm", EXPERTS * HM // 2), signal("hid_ready", EXPERTS * HM // 2)
        y_mm, y_taken = signal("y_mm", EXPERTS), signal("y_taken", EXPERTS)
        h3_ready, h3_used = signal("h3_ready"), signal("h3_used")
        t_b, tc_b = signal("t_b", 3), signal("tc_b", 3)
        xz_mm, xpad_ready, z_ready = signal("xz_mm"), signal("xpad_ready"), signal("z_ready")
        uc_ready, u_ready = signal("uc_ready"), signal("u_ready")
        bc_mm, bc_in, bc_out, bc3_ready = signal("bc_mm"), signal("bc_in"), signal("bc_out"), signal("bc3_ready")
        dtp_mm, dtp_ready, dt_mm = signal("dtp_mm"), signal("dtp_ready"), signal("dt_mm")
        relu_ready, sp_ready, delta_ready, du_ready = (signal("relu_ready"), signal("sp_ready"),
                                                       signal("delta_ready"), signal("du_ready"))
        STEPS = STATE // 2 * CH
        bcast_mm = signal("bcast_mm", STATE // 2)
        dA_ready, dbu_ready, scan_ready, hc_ready, y_added = (signal(n, STEPS) for n in (
            "dA_ready", "dbu_ready", "scan_ready", "hc_ready", "y_added"))
        yz_ready, out_mm = signal("yz_ready"), signal("out_mm")
        var_b, rstd_b = signal("var_b", 2), signal("rstd_b", 2)
        h4_ready, gate1_mm, th_ready = signal("h4_ready"), signal("gate1_mm"), signal("th_ready")
        f13_mm, sg_ready, gg_ready, fy_mm, fy_taken = (signal(n, FFN) for n in (
            "f13_mm", "sg_ready", "gg_ready", "fy_mm", "fy_taken"))
        fin_ready, fin_free = signal("fin_ready"), signal("fin_free", 16)
        abs_done, exp_done = signal("abs_done"), signal("exp_done")
        pair_added = signal("pair_added", STEPS - CH)
        exp_a, neg_a, tokw_part = signal("exp_a"), signal("neg_a"), signal("tokw_part")
        dve_f, dve_b = signal("dve_f", 44), signal("dve_b", 49)

        block = ctx.enter_context(nc.Block())

        @block.sync
        def _(sp):
            def load(name, *pairs):
                for dst, src in pairs:
                    sp.dma_start(dst, src).then_inc(ld[name].sem, 16)

            def load_x(i):
                sp.dma_start(xb[:, :, :].rearrange("p k t -> p (k t)"),
                             d["x"][bass.ds(i, 1), :, :].rearrange("a p n -> (a p) n")
                             ).then_inc(x_loaded.sem, 16)

            def store(i):
                sp.wait_ge(fin_ready.sem, fin_ready.at(i, 1))
                sp.dma_start(out[bass.ds(i, 1), :, :, :].rearrange("a u p e -> (a p) u e"), fin[:, :, :]
                             ).then_inc(fin_free.sem, 16)

            def load_experts(i):
                for e in range(EXPERTS + 1):
                    if e < EXPERTS:
                        if e >= 2:
                            sp.wait_ge(hid_mm.sem, hid_mm.at(i, (e - 1) * HM // 2))
                        elif not first(i):
                            sp.wait_ge(hid_mm.sem, hid_mm.at(i, 0))
                        sp.dma_start(w1[e % 2][:, :, :], d["w1"][e, :, :, :]).then_inc(w1_loaded[e % 2].sem, 16)
                    if e:
                        p = e - 1
                        if p >= 2:
                            sp.wait_ge(y_mm.sem, y_mm.at(i, p - 1))
                        elif not first(i):
                            sp.wait_ge(y_mm.sem, y_mm.at(i, 0))
                        sp.dma_start(w2[p % 2][:, :, :], d["w2"][p, :, :, :]).then_inc(w2_loaded[p % 2].sem, 16)

            sp.sem_inc(fin_free.sem, 16)
            load("cst", (cst[:, :], d["cst"]), (tokgb[:, :, :, :], d["tokgb"]))
            for s in range(SHIFTS):
                load("tok", (wraw[:, s, :, :], d["tok_w"][:, s, :, :]))
            load_x(0)
            load("rows", (rows[:, :], d["rows"].partition_broadcast(P)), (ln12[:, :], d["ln12"]),
                 (cols[:, :, :], d["cols"]), (b1[:, :], d["b1"]))
            load("attn1", (qkv_w[0][:, :, :], d["qkv1"]), (proj_w[0][:, :, :], d["proj1"]))
            load("attn2", (qkv_w[1][:, :, :], d["qkv2"]), (proj_w[1][:, :, :], d["proj2"]))
            load("gate0", (gate0_w[:, :, :], d["gate0"]), (b2[:, :], d["b2"]))
            load("scan", (in_w[:, :, :], d["in_w"]), (x_w[:, :, :], d["x_w"]),
                 (dt_w[:, :, :], d["dt_w"]), (out_w[:, :, :], d["out_w"]))
            load("ffn", (gate1_w[:, :, :], d["gate1"]), (f1_w[:, :, :], d["f1"]), (f3_w[:, :, :], d["f3"]),
                 (f2_w[:, :, :], d["f2"]))
            sp.wait_ge(tok_mm.sem, tok_mm.at(0, 2))
            load_x(1)
            load_experts(0)
            with sp.Fori(1, BLOCKS - 1) as i:
                sp.wait_ge(tok_mm.sem, tok_mm.at(i, 2))
                load_x(i + 1)
                load_experts(i)
                store(i - 1)
            load_experts(BLOCKS - 1)
            store(BLOCKS - 2)
            store(BLOCKS - 1)
            sp.wait_ge(fin_free.sem, fin_free.at(BLOCKS, 16))

        @block.tensor
        def _(pe):
            def mm(o, l, r, first=True, last=True):
                return nc.tensor.matmul(o, l, r, start=first, stop=last)

            def turn(src, dst, sig):
                for h in range(2):
                    for u in range(U):
                        ins = nc.tensor.transpose(dst[0:HALF, h * BT + u * P:h * BT + (u + 1) * P],
                                                  src[:, u, h * HALF:(h + 1) * HALF], ident)
                ins.then_inc(sig.sem, 1)

            def loaded(name, n):
                pe.wait_ge(ld[name].sem, 16 * n)

            loaded("cst", 2)
            loaded("tok", SHIFTS)
            pe.wait_ge(ready.sem, 1)
            for s in range(SHIFTS):
                for k in range(PK):
                    ins = mm(A[:, 0:DIM], tokgb[:, 1, s, k:k + 1].broadcast_to([PR, P]), wraw[:, s, k, :],
                             s == 0 and k == 0, s == SHIFTS - 1 and k == PK - 1)
            ins.then_inc(beta_mm.sem, 1)
            pe.wait_ge(tokw_ready.sem, 1)
            for k in range(PK):
                ins = mm(B[:, 0:DIM], ones[0:PR, :], tokw[:, k, 0:DIM], k == 0, k == PK - 1)
            ins.then_inc(colsum_mm.sem, 1)
            for name, n in (("attn1", 2), ("attn2", 2)):
                loaded(name, n)

            def tok(i):
                pe.wait_ge(x_loaded.sem, x_loaded.at(i, 16))
                pe.wait_ge(ready.sem, 2)
                for u in range(U):
                    for k in range(PK):
                        ins = mm(A[:, u * (DIM + 1):(u + 1) * (DIM + 1)], xb[:, k, u * P:(u + 1) * P],
                                 tokw[:, k, :], k == 0, k == PK - 1)
                ins.then_inc(tok_mm.sem, 1)
                pe.wait_ge(sq_ready.sem, sq_ready.at(i, 1))
                for u in range(U):
                    for k in range(PK):
                        ins = mm(B[:, u:u + 1], sq[:, k, u * P:(u + 1) * P], cnt[:, k:k + 1],
                                 k == 0, k == PK - 1)
                ins.then_inc(tok_mm.sem, 1)

            def qkv(n, i):
                pe.wait_ge(h_f.sem, h_f.at(i, n + 1))
                turn((h0, z)[n], C, t_f)
                pe.wait_ge(tc_f.sem, tc_f.at(i, 2 * n + 1))
                for part, b in ((0, A), (1, B)):
                    for m in range(2):
                        for kk in range(2):
                            mm(b[0:HALF, m * BT:(m + 1) * BT],
                               qkv_w[n][:, kk, part * DIM + m * HALF:part * DIM + (m + 1) * HALF],
                               hT[:, kk, :], kk == 0, kk == 1)
                for u in range(U):
                    for kk in range(2):
                        ins = mm(D[:, u * DIM:(u + 1) * DIM], hT[:, kk, u * P:(u + 1) * P],
                                 qkv_w[n][:, kk, 2 * DIM:3 * DIM], kk == 0, kk == 1)
                ins.then_inc(qkv_mm.sem, 1)

            def scores(n, i):
                pe.wait_ge(q_ready.sem, q_ready.at(i, n + 1))
                pe.wait_ge(kx_ready.sem, kx_ready.at(i, n + 1))
                for u, b in ((0, A), (1, B)):
                    for g in range(4):
                        at = u * P + 32 * g
                        for m in range(2):
                            ins = mm(b[32 * g:32 * g + 32, m * HH * 32:(m + 1) * HH * 32],
                                     qT[:, m, at:at + 32], kx[:, m, :, at:at + 32])
                ins.then_inc(s_mm.sem, 1)

            def values(n, i):
                pe.wait_ge(pbd_ready.sem, pbd_ready.at(i, n + 1))
                pe.wait_ge(v_ready.sem, v_ready.at(i, n + 1))
                for u in range(U):
                    for h in range(HEADS):
                        ins = mm(C[:, u * DIM + h * HD:u * DIM + (h + 1) * HD], pbd[:, u * HEADS + h, :],
                                 vt[:, u, h * HD:(h + 1) * HD])
                ins.then_inc(pv_mm.sem, 1)

            def project(n, i):
                pe.wait_ge(o_ready.sem, o_ready.at(i, n + 1))
                turn(ot, A, t_f)
                pe.wait_ge(tc_f.sem, tc_f.at(i, 2 * n + 2))
                for u in range(U):
                    for kk in range(2):
                        ins = mm(B[:, u * DIM:(u + 1) * DIM], oT[:, kk, u * P:(u + 1) * P],
                                 proj_w[n][:, kk, :], kk == 0, kk == 1)
                ins.then_inc(proj_mm.sem, 1)


            def gate(i):
                if isinstance(i, int):
                    loaded("gate0", 2)
                pe.wait_ge(h_f.sem, h_f.at(i, 3))
                turn(z, C, t_f)
                pe.wait_ge(tc_f.sem, tc_f.at(i, 5))
                for u in range(U):
                    for kk in range(2):
                        ins = mm(D[:, u * 8:u * 8 + 8], h2T[:, kk, u * P:(u + 1) * P], gate0_w[:, kk, :],
                                 kk == 0, kk == 1)
                ins.then_inc(gate_mm.sem, 1)

            def gate_bias(i):
                pe.wait_ge(cw_ready.sem, cw_ready.at(i, 1))
                for u in range(U):
                    ins = nc.tensor.transpose(D[0:8, u * P:(u + 1) * P], cw[:, u, :], ident)
                ins.then_inc(cwT_mm.sem, 1)
                pe.wait_ge(cwT_ready.sem, cwT_ready.at(i, 1))
                for u in range(U):
                    ins = mm(C[:, u * DIM:(u + 1) * DIM], cwT[:, u * P:(u + 1) * P], b2[:, :])
                ins.then_inc(b2_mm.sem, 1)

            def hidden(e, i):
                pe.wait_ge(w1_loaded[e % 2].sem, w1_loaded[e % 2].at(i, 16 * (e // 2 + 1)))
                for mp in range(HM // 2):
                    unit = e * HM // 2 + mp
                    if unit >= 2:
                        pe.wait_ge(hid_ready.sem, hid_ready.at(i, unit - 1))
                    b = (A, B)[unit % 2]
                    for m in range(2):
                        at = (2 * mp + m) * P
                        for kk in range(2):
                            ins = mm(b[:, m * BT:(m + 1) * BT], w1[e % 2][:, kk, at:at + P], h2T[:, kk, :],
                                     kk == 0, kk == 1)
                    ins.then_inc(hid_mm.sem, 1)

            def expert_out(e, i):
                pe.wait_ge(w2_loaded[e % 2].sem, w2_loaded[e % 2].at(i, 16 * (e // 2 + 1)))
                pe.wait_ge(hid_ready.sem, hid_ready.at(i, (e + 1) * HM // 2))
                if e < 2:
                    pe.wait_ge(acc0_ready.sem, acc0_ready.at(i, 1))
                else:
                    pe.wait_ge(y_taken.sem, y_taken.at(i, e - 1))
                b = (D, C)[e % 2]
                for u in range(U):
                    for m in range(HM):
                        ins = mm(b[:, u * DIM:(u + 1) * DIM], he[e % 2][:, m, u * P:(u + 1) * P],
                                 w2[e % 2][:, m, :], m == 0, m == HM - 1)
                ins.then_inc(y_mm.sem, 1)

            def xz(i):
                loaded("scan", 4)
                loaded("ffn", 4)
                pe.wait_ge(h3_ready.sem, h3_ready.at(i, 1))
                if isinstance(i, int):
                    if not first(i):
                        pe.wait_ge(fy_taken.sem, fy_taken.at(i, 0))
                turn(h3, Q[3], t_b)
                pe.wait_ge(tc_b.sem, tc_b.at(i, 1))
                for m in range(2 * CH):
                    for kk in range(2):
                        ins = mm(Q[m // 2][:, (m % 2) * BT:(m % 2 + 1) * BT], in_w[:, kk, m * P:(m + 1) * P],
                                 h3T[:, kk, :], kk == 0, kk == 1)
                ins.then_inc(xz_mm.sem, 1)

            def bc_dt(i):
                pe.wait_ge(u_ready.sem, u_ready.at(i, 1))
                for u in range(U):
                    for c in range(CH):
                        ins = mm(Q[3][:, u * 32:(u + 1) * 32], uu[:, c, u * P:(u + 1) * P],
                                 x_w[:, c, 0:32], c == 0, c == CH - 1)
                ins.then_inc(bc_mm.sem, 1)
                for m in range(CH):
                    for c in range(CH):
                        ins = mm(Q[m // 2][:, (m % 2) * BT:(m % 2 + 1) * BT],
                                 x_w[:, c, 32 + m * P:32 + (m + 1) * P], uu[:, c, :], c == 0, c == CH - 1)
                ins.then_inc(dtp_mm.sem, 1)

            def dt_bcT(i):
                pe.wait_ge(dtp_ready.sem, dtp_ready.at(i, 1))
                for m in range(CH):
                    b, at = (Q[2], m * BT) if m < 2 else (Q[0], 0)
                    for c in range(CH):
                        ins = mm(b[:, at:at + BT], dt_w[:, c, m * P:(m + 1) * P], dtp[:, c, :],
                                 c == 0, c == CH - 1)
                ins.then_inc(dt_mm.sem, 1)
                pe.wait_ge(bc3_ready.sem, bc3_ready.at(i, 1))
                for u in range(U):
                    ins = nc.tensor.transpose(q1b[0:HALF, u * P:(u + 1) * P],
                                              bc3[:, u, :, :].rearrange("p a s -> p (a s)"), identb[:, :])
                ins.then_inc(t_b.sem, 1)

            q1b = Q[1][:, :].bitcast(BF16)

            def spread(sp2, i):
                if sp2 == 0:
                    pe.wait_ge(tc_b.sem, tc_b.at(i, 2))
                    pe.wait_ge(delta_ready.sem, delta_ready.at(i, 1))
                if sp2 >= 2:
                    pe.wait_ge(hc_ready.sem, hc_ready.at(i, CH * (sp2 - 1)))
                for part, b in ((0, Q[sp2 % 2]), (STATE, Q[2 + sp2 % 2])):
                    for k in range(2):
                        s = part + 2 * sp2 + k
                        ins = mm(b[:, k * BT:(k + 1) * BT], pick[:, s:s + 1].broadcast_to([HALF, P]),
                                 bcT[:, :])
                ins.then_inc(bcast_mm.sem, 1)

            def scan_out(i):
                pe.wait_ge(yz_ready.sem, yz_ready.at(i, 1))
                for u in range(U):
                    for c in range(CH):
                        ins = mm(Q[0][:, u * DIM:(u + 1) * DIM], yy[:, c, u * P:(u + 1) * P], out_w[:, c, :],
                                 c == 0, c == CH - 1)
                ins.then_inc(out_mm.sem, 1)

            def gate1(i):
                pe.wait_ge(h4_ready.sem, h4_ready.at(i, 1))
                turn(h4, Q[1], t_b)
                pe.wait_ge(tc_b.sem, tc_b.at(i, 3))
                for u in range(U):
                    for kk in range(2):
                        ins = mm(Q[2][:, u * 8:u * 8 + 8], h4T[:, kk, u * P:(u + 1) * P], gate1_w[:, kk, :],
                                 kk == 0, kk == 1)
                ins.then_inc(gate1_mm.sem, 1)

            def ffn_in(e, i):
                if e >= 2:
                    pe.wait_ge(gg_ready.sem, gg_ready.at(i, e - 1))
                b = (Q[0], Q[3])[e % 2]
                for at, w in ((0, f1_w), (BT, f3_w)):
                    for kk in range(2):
                        ins = mm(b[:, at:at + BT], w[:, kk, e * INTER:(e + 1) * INTER], h4T[:, kk, :],
                                 kk == 0, kk == 1)
                ins.then_inc(f13_mm.sem, 1)

            def ffn_out(e, i):
                pe.wait_ge(gg_ready.sem, gg_ready.at(i, e + 1))
                if e >= 2:
                    pe.wait_ge(fy_taken.sem, fy_taken.at(i, e - 1))
                b = (Q[1], Q[2])[e % 2]
                for u in range(U):
                    ins = mm(b[:, u * DIM:(u + 1) * DIM], gg[e % 2][:, u * P:(u + 1) * P], f2_w[:, e, :])
                ins.then_inc(fy_mm.sem, 1)

            def step(i, b):
                if i is not None:
                    tok(i)
                    qkv(0, i)
                if b is not None:
                    xz(b)
                if i is not None:
                    scores(0, i)
                if b is not None:
                    bc_dt(b)
                if i is not None:
                    values(0, i)
                if b is not None:
                    dt_bcT(b)
                if i is not None:
                    project(0, i)
                    qkv(1, i)
                    scores(1, i)
                    values(1, i)
                    project(1, i)
                    gate(i)
                    gate_bias(i)
                for e in range(EXPERTS + 1):
                    if i is not None and e < EXPERTS:
                        hidden(e, i)
                    if b is not None and e < EXPERTS:
                        spread(e, b)
                    if i is not None and e:
                        expert_out(e - 1, i)
                if b is not None:
                    scan_out(b)
                    gate1(b)
                    for e in range(FFN + 1):
                        if e < FFN:
                            ffn_in(e, b)
                        if e:
                            ffn_out(e - 1, b)

            step(0, None)
            with pe.Fori(1, BLOCKS) as i:
                step(i, i - 1)
            step(None, BLOCKS - 1)

        @block.scalar
        def _(act):
            def copy(dst, src, sig, **kw):
                act.activation(dst, src, ACT.Copy if not kw else ACT.Identity, **kw).then_inc(sig.sem, 1)

            act.wait_ge(ld["cst"].sem, 32)
            act.wait_ge(ld["rows"].sem, 64)

            def squares(i):
                act.wait_ge(x_loaded.sem, x_loaded.at(i, 16))
                if not first(i):
                    act.wait_ge(y_mm.sem, y_mm.at(i, 0))
                act.activation(sq[:, :, :], xb[:, :, :], ACT.Square).then_inc(sq_ready.sem, 1)

            def turned(bank_, dst, k, ln, i):
                act.wait_ge(t_f.sem, t_f.at(i, k))
                src = bank_[0:HALF, :].rearrange("p (h t) -> p h t", h=2)
                if ln is None:
                    act.activation(dst[:, :, :], src, ACT.Copy).then_inc(tc_f.sem, 1)
                else:
                    for h in range(2):
                        ins = act.activation(dst[:, h, :], src[:, h, :], ACT.Identity,
                                             scale=ln12[:, 4 * ln + h:4 * ln + h + 1],
                                             bias=ln12[:, 4 * ln + 2 + h:4 * ln + 3 + h])
                    ins.then_inc(tc_f.sem, 1)

            def values(n, i):
                act.wait_ge(qkv_mm.sem, qkv_mm.at(i, n + 1))
                act.activation(vt[:, :, :], D[:, 0:U * DIM].rearrange("p (u e) -> p u e", u=U), ACT.Copy
                               ).then_inc(v_ready.sem, 1)
                if n == 1:
                    act.activation(qT[:, :, :], A[0:HALF, :].rearrange("p (m t) -> p m t", m=2), ACT.Copy
                                   ).then_inc(q_ready.sem, 1)
                    act.activation(kT[:, :, :], B[0:HALF, :].rearrange("p (m t) -> p m t", m=2), ACT.Copy
                                   ).then_inc(k_ready.sem, 1)

            def heads_out(i):
                act.wait_ge(pv_mm.sem, pv_mm.at(i, 1))
                act.activation(ot[:, :, :], C[:, 0:U * DIM].rearrange("p (u e) -> p u e", u=U), ACT.Copy
                               ).then_inc(o_ready.sem, 1)

            def softmax_exp(i):
                act.wait_ge(sm_in.sem, sm_in.at(i, 1))
                act.activation(pm[:, :, :, :], pm[:, :, :, :], ACT.Exp, scale=HD ** -0.5
                               ).then_inc(sm_out.sem, 1)

            def gate_exp(i):
                act.wait_ge(gate_in.sem, gate_in.at(i, 1))
                act.activation(ge[:, :, :], gd[:, :, :], ACT.Exp).then_inc(gate_out.sem, 1)

            def gelu(e, i):
                if e >= 2:
                    act.wait_ge(y_mm.sem, y_mm.at(i, e - 1))
                for mp in range(HM // 2):
                    unit = e * HM // 2 + mp
                    act.wait_ge(hid_mm.sem, hid_mm.at(i, unit + 1))
                    b = (A, B)[unit % 2]
                    for m in range(2):
                        at = 2 * mp + m
                        ins = act.activation(he[e % 2][:, at, :], b[:, m * BT:(m + 1) * BT], ACT.Gelu,
                                             bias=b1[:, e * HM + at:e * HM + at + 1])
                    ins.then_inc(hid_ready.sem, 1)

            def h3_turned(i):
                act.wait_ge(t_b.sem, t_b.at(i, 1))
                act.activation(h3T[:, :, :], Q[3][0:HALF, :].rearrange("p (h t) -> p h t", h=2), ACT.Copy
                               ).then_inc(tc_b.sem, 1)

            def xz(i):
                act.wait_ge(xz_mm.sem, xz_mm.at(i, 1))
                for c in range(CH):
                    src = Q[c // 2][:, (c % 2) * BT:(c % 2 + 1) * BT].rearrange("p (b n) -> p b n", b=BI)
                    ins = act.activation(xpad[:, c, :, TAPS - 1:], src, ACT.Copy)
                ins.then_inc(xpad_ready.sem, 1)
                for c in range(CH):
                    m = CH + c
                    ins = act.activation(sz[:, c, :], Q[m // 2][:, (m % 2) * BT:(m % 2 + 1) * BT], ACT.Silu)
                ins.then_inc(z_ready.sem, 1)

            def u_silu(i):
                act.wait_ge(uc_ready.sem, uc_ready.at(i, 1))
                for c in range(CH):
                    ins = act.activation(uu[:, c, :], uc[:, c, :], ACT.Silu,
                                         bias=cols[:, c, TAPS:TAPS + 1])
                ins.then_inc(u_ready.sem, 1)

            def scan_inputs(i):
                xz(i)
                u_silu(i)

            def dt_first(i):
                act.wait_ge(dtp_mm.sem, dtp_mm.at(i, 1))
                act.activation(dtp[:, 0:2, :], Q[0][:, :].rearrange("p (m t) -> p m t", m=2), ACT.Copy)
                act.activation(dtp[:, 2, :], Q[1][:, 0:BT], ACT.Copy).then_inc(dtp_ready.sem, 1)
                act.wait_ge(bc_in.sem, bc_in.at(i, 1))
                act.activation(be[:, :, :], bd[:, :, :], ACT.Exp).then_inc(bc_out.sem, 1)

            def softplus(i):
                act.wait_ge(dt_mm.sem, dt_mm.at(i, 1))
                for m in range(CH):
                    b, at = (Q[2], m * BT) if m < 2 else (Q[0], 0)
                    act.activation(delta[:, m, :], b[:, at:at + BT], ACT.Relu,
                                   bias=cols[:, m, TAPS + 1:TAPS + 2])
                    ins = act.activation(dab[:, m, :], b[:, at:at + BT], ACT.Abs,
                                         bias=cols[:, m, TAPS + 1:TAPS + 2])
                ins.then_inc(abs_done.sem, 1)
                act.wait_ge(abs_done.sem, abs_done.at(i, 1))
                act.activation(dab[:, :, :], dab[:, :, :], ACT.Exp, scale=-1.0).then_inc(exp_done.sem, 1)
                act.wait_ge(exp_done.sem, exp_done.at(i, 1))
                act.activation(dab[:, :, :], dab[:, :, :], ACT.Ln, bias=1.0).then_inc(sp_ready.sem, 1)
                act.wait_ge(t_b.sem, t_b.at(i, 2))
                act.activation(bcT[:, :], q1b[0:HALF, 0:BT], ACT.Copy).then_inc(tc_b.sem, 1)

            q1b = Q[1][:, :].bitcast(BF16)

            def decays(sp2, i):
                if sp2 == 0:
                    act.wait_ge(delta_ready.sem, delta_ready.at(i, 1))
                for c in range(CH):
                    n = sp2 * CH + c
                    if n >= 3:
                        act.wait_ge(scan_ready.sem, scan_ready.at(i, n - 2))
                    for k in range(2):
                        s = 2 * sp2 + k
                        ins = act.activation(
                            dA[n % 3][:, k * BI:(k + 1) * BI, 1:],
                            delta[:, c, :].rearrange("p (b n) -> p b n", b=BI)[:, :, 1:], ACT.Exp,
                            scale=decay[:, c, s:s + 1])
                    ins.then_inc(dA_ready.sem, 1)

            def h4_turned(i):
                act.wait_ge(t_b.sem, t_b.at(i, 3))
                act.activation(h4T[:, :, :], Q[1][0:HALF, :].rearrange("p (h t) -> p h t", h=2), ACT.Copy
                               ).then_inc(tc_b.sem, 1)

            def gate1_tanh(i):
                act.wait_ge(gate1_mm.sem, gate1_mm.at(i, 1))
                act.activation(th[:, :, :], Q[2][:, 0:16].rearrange("p (u e) -> p u e", u=U), ACT.Tanh, scale=0.5
                               ).then_inc(th_ready.sem, 1)

            def ffn_silu(e, i):
                act.wait_ge(f13_mm.sem, f13_mm.at(i, e + 1))
                if e >= 2:
                    act.wait_ge(gg_ready.sem, gg_ready.at(i, e - 1))
                act.activation(sg[e % 2][:, :], (Q[0], Q[3])[e % 2][:, 0:BT], ACT.Silu
                               ).then_inc(sg_ready.sem, 1)

            act.activation(decay[:, :, :], cols[:, :, TAPS + 2:], ACT.Exp).then_inc(exp_a.sem, 1)
            act.wait_ge(neg_a.sem, 1)

            def step(i, b):
                if i is not None:
                    squares(i)
                    turned(C, hT, 1, None, i)
                if b is not None:
                    h3_turned(b)
                if i is not None:
                    values(0, i)
                if b is not None:
                    scan_inputs(b)
                if i is not None:
                    heads_out(i)
                if b is not None:
                    dt_first(b)
                if i is not None:
                    turned(A, oT, 2, None, i)
                if b is not None:
                    softplus(b)
                if i is not None:
                    turned(C, hT, 3, 0, i)
                    values(1, i)
                    softmax_exp(i)
                    turned(A, oT, 4, None, i)
                    turned(C, h2T, 5, 1, i)
                    gate_exp(i)
                for e in range(EXPERTS):
                    if i is not None:
                        gelu(e, i)
                    if b is not None:
                        decays(e, b)
                if b is not None:
                    h4_turned(b)
                    gate1_tanh(b)
                    for e in range(FFN):
                        ffn_silu(e, b)

            step(0, None)
            with act.Fori(1, BLOCKS) as i:
                step(i, i - 1)
            step(None, BLOCKS - 1)

        @block.vector
        def _(dve):
            V = nc.vector
            cf, cb = Chain(dve, dve_f), Chain(dve, dve_b)

            V.memset(ones[:, :], 1.0)
            V.memset(half_neg[:, :], -0.5)
            for n in range(3):
                V.memset(dA[n][:, :, 0:1], 0.0)
            V.memset(xpad[:, :, :, 0:TAPS - 1], 0.0)
            dve.wait_ge(ld["cst"].sem, 32)
            V.tensor_copy(tokw[:, :, DIM:DIM + 1], cnt.unsqueeze(2))
            V.tensor_copy(identb[:, :], ident)
            for part in range(3):
                V.tensor_copy(pick[32 * part:32 * part + 32, :], ident[0:32, 0:32])
            V.memset(pbd[:, :, :], 0.0).then_inc(ready.sem, 1)
            dve.wait_ge(ld["tok"].sem, 16 * SHIFTS)
            for s in range(SHIFTS):
                for k in range(PK):
                    gain, w, o = tokgb[:, 0, s, k:k + 1], wraw[:, s, k, :], tokw[:, k, 0:DIM]
                    if s == 0:
                        ins = V.tensor_scalar(o, w, gain, None, ALU.mult)
                    else:
                        ins = V.scalar_tensor_tensor(out=o, in0=w, scalar=gain, in1=o, op0=ALU.mult, op1=ALU.add)
                if s < SHIFTS - 1:
                    ins.then_inc(tokw_part.sem, 1)
                    dve.wait_ge(tokw_part.sem, s + 1)
            ins.then_inc(tokw_ready.sem, 1)
            dve.wait_ge(ld["rows"].sem, 64)
            dve.wait_ge(beta_mm.sem, 1)
            V.tensor_tensor(tok_bw[:, :], A[:, 0:DIM], tok_b, ALU.add)
            dve.wait_ge(colsum_mm.sem, 1)
            V.tensor_copy(tok_cs[:, :], B[:, 0:DIM]).then_inc(ready.sem, 1)
            dve.wait_ge(ready.sem, 2)
            dve.wait_ge(exp_a.sem, 1)
            V.tensor_scalar(decay[:, :, :], decay[:, :, :], -1.0, None, ALU.mult).then_inc(neg_a.sem, 1)

            def norm(i, ch, src, dst, k, var, rs, bufs, done):
                st_, mv_, ve_, rstd_ = bufs
                for u in range(U):
                    n = ch.step(V.bn_stats(st_[:, u, :], src[:, u, :]))
                ch.after(n)
                V.memset(idle[:, :], 0.0)
                for u in range(U):
                    n = ch.step(V.bn_aggr(mv_[:, u, :], st_[:, u, :]))
                ch.after(n)
                V.tensor_scalar(ve_[:, :], mv_[:, :, 1], EPS, None, ALU.add).then_inc(var.sem, 1)
                dve.wait_ge(rs.sem, rs.at(i, k))
                for u in range(U):
                    ins = V.tensor_scalar(dst[:, u, :], src[:, u, :], mv_[:, u, 0:1], rstd_[:, u:u + 1],
                                          ALU.subtract, ALU.mult)
                if done is None:
                    ch.link(ins)
                else:
                    ins.then_inc(done.sem, 1)

            fb, bb = (st, mv, ve, rstd), (stb, mvb, veb, rstdb)

            def two(ap):
                return ap.rearrange("p (u e) -> p u e", u=U)

            def tok(i):
                cf.start(i)
                if not first(i):
                    dve.wait_ge(h3_ready.sem, h3_ready.at(i, 0))
                dve.wait_ge(tok_mm.sem, tok_mm.at(i, 2))
                sums = A[:, DIM:2 * (DIM + 1):DIM + 1]
                cf.link(V.tensor_scalar(mv[:, :, 0], sums, -1.0 / PATCH_DIM, None, ALU.mult))
                cf.link(V.tensor_tensor(mv[:, :, 1], mv[:, :, 0], mv[:, :, 0], ALU.mult))
                cf.link(V.scalar_tensor_tensor(out=ve[:, :], in0=B[:, 0:U], scalar=1.0 / PATCH_DIM,
                                               in1=mv[:, :, 1], op0=ALU.mult, op1=ALU.subtract))
                V.tensor_scalar(ve[:, :], ve[:, :], EPS, None, ALU.add).then_inc(var_f.sem, 1)
                for u in range(U):
                    n = cf.step(V.scalar_tensor_tensor(
                        out=tmp[:, u, :], in0=tok_cs[:, :], scalar=mv[:, u, 0:1],
                        in1=A[:, u * (DIM + 1):u * (DIM + 1) + DIM], op0=ALU.mult, op1=ALU.add))
                cf.after(n)
                dve.wait_ge(rstd_f.sem, rstd_f.at(i, 1))
                for u in range(U):
                    ins = V.scalar_tensor_tensor(out=h0[:, u, :], in0=tmp[:, u, :], scalar=rstd[:, u:u + 1],
                                                 in1=tok_bw[:, :], op0=ALU.mult, op1=ALU.add)
                ins.then_inc(h_f.sem, 1)

            def qk_l1(i):
                dve.wait_ge(qkv_mm.sem, qkv_mm.at(i, 1))
                for n, b in ((0, A), (1, B)):
                    last = cf.step(V.tensor_reduce(
                        l1[:, :, n * BI:(n + 1) * BI], b[0:HALF, :].rearrange("p (m b n) -> p m b n", m=2, b=BI),
                        AX.X, ALU.add, apply_absolute_value=True))
                cf.after(last)
                cf.link(V.tensor_scalar(l1[:, :, :], l1[:, :, :], 1e-12, None, ALU.max))
                cf.link(V.reciprocal(l1[:, :, :], l1[:, :, :]))
                for n, b, o, sig in ((1, B, kT, k_ready), (0, A, qT, q_ready)):
                    for m in range(2):
                        ins = V.tensor_tensor(
                            o[:, m, :].rearrange("p (b n) -> p b n", b=BI),
                            b[0:HALF, m * BT:(m + 1) * BT].rearrange("p (b n) -> p b n", b=BI),
                            l1[:, m, n * BI:(n + 1) * BI].unsqueeze(2).broadcast_to([HALF, BI, SEQ]), ALU.mult)
                    ins.then_inc(sig.sem, 1)

            def to_block_diagonal():
                for g in range(4):
                    r = slice(32 * g, 32 * g + 32)
                    ins = V.transpose(pbd[r, :, r], pm[r, :, :, :].rearrange("p u h j -> p (u h) j"))
                ins.then_inc(pbd_ready.sem, 1)

            def linear_mask(i):
                dve.wait_ge(s_mm.sem, s_mm.at(i, 1))
                for u, b in ((0, A), (1, B)):
                    n = cf.step(V.tensor_tensor(
                        pm[:, u, :, :], b[:, 0:HEADS * 32].rearrange("p (h j) -> p h j", h=HEADS),
                        mask.unsqueeze(1).broadcast_to([P, HEADS, 32]), ALU.mult))
                cf.after(n)
                to_block_diagonal()

            def after_linear(i):
                dve.wait_ge(proj_mm.sem, proj_mm.at(i, 1))
                dve.wait_ge(h0b_ready.sem, h0b_ready.at(i, 1))
                cf.link(V.tensor_tensor(tmp[:, :, :], two(B[:, 0:U * DIM]), hb[:, :, :], ALU.add))
                norm(i, cf, tmp, h1, 2, var_f, rstd_f, fb, h1_ready)
                dve.wait_ge(h1_ready.sem, h1_ready.at(i, 1))
                norm(i, cf, h1, z, 3, var_f, rstd_f, fb, h_f)

            def softmax(i):
                dve.wait_ge(s_mm.sem, s_mm.at(i, 2))
                for u, b in ((0, A), (1, B)):
                    n = cf.step(V.tensor_tensor(
                        pm[:, u, :, :], b[:, 0:HEADS * 32].rearrange("p (h j) -> p h j", h=HEADS),
                        neg.unsqueeze(1).broadcast_to([P, HEADS, 32]), ALU.add))
                cf.after(n)
                flat = pm[:, :, :, :].rearrange("p u h j -> p (u h) j")
                cf.link(V.tensor_reduce(mx[:, :], flat, AX.X, ALU.max))
                V.tensor_tensor(flat, flat, mx[:, :].unsqueeze(2).broadcast_to([P, U * HEADS, 32]),
                                ALU.subtract).then_inc(sm_in.sem, 1)
                dve.wait_ge(sm_out.sem, sm_out.at(i, 1))
                to_block_diagonal()
                cf.link(V.tensor_reduce(mx[:, :], flat, AX.X, ALU.add))
                cf.link(V.reciprocal(mx[:, :], mx[:, :]))

            def heads_out(i):
                dve.wait_ge(pv_mm.sem, pv_mm.at(i, 2))
                V.tensor_tensor(ot[:, :, :].rearrange("p u (h d) -> p (u h) d", h=HEADS),
                                C[:, 0:U * DIM].rearrange("p (x d) -> p x d", d=HD),
                                mx[:, :].unsqueeze(2).broadcast_to([P, U * HEADS, HD]), ALU.mult
                                ).then_inc(o_ready.sem, 1)

            def after_softmax(i):
                dve.wait_ge(proj_mm.sem, proj_mm.at(i, 2))
                dve.wait_ge(h1b_ready.sem, h1b_ready.at(i, 1))
                V.tensor_tensor(xm[:, :, :], two(B[:, 0:U * DIM]), hb[:, :, :], ALU.add).then_inc(xm_ready.sem, 1)
                dve.wait_ge(xm_ready.sem, xm_ready.at(i, 1))
                norm(i, cf, xm, z, 4, var_f, rstd_f, fb, h_f)

            def ranks(ch, vals, n, rk_, req_, rank_):
                a = vals.unsqueeze(2).broadcast_to([P, U, n, n])
                b = vals.unsqueeze(3).broadcast_to([P, U, n, n])
                ch.step(V.tensor_tensor(rk_[:, :, 0:n, 0:n], a, b, ALU.is_gt))
                ch.link(V.tensor_tensor(req_[:, :, 0:n, 0:n], a, b, ALU.is_equal))
                ch.link(V.tensor_tensor(req_[:, :, 0:n, 0:n], req_[:, :, 0:n, 0:n],
                                        tri[:, 0:n, 0:n].unsqueeze(1).broadcast_to([P, U, n, n]), ALU.mult))
                ch.link(V.tensor_tensor(rk_[:, :, 0:n, 0:n], rk_[:, :, 0:n, 0:n], req_[:, :, 0:n, 0:n], ALU.add))
                ch.link(V.tensor_reduce(rank_[:, :, 0:n], rk_[:, :, 0:n, 0:n], AX.X, ALU.add))
                ch.link(V.tensor_scalar(rank_[:, :, 0:n], rank_[:, :, 0:n], 1.5, None, ALU.is_lt))

            def over8(ap):
                return ap.broadcast_to([P, U, 8])

            def gate(i):
                dve.wait_ge(gate_mm.sem, gate_mm.at(i, 1))
                cf.link(V.tensor_tensor(lg[:, :, :], two(D[:, 0:16]), gate0_b.unsqueeze(1).broadcast_to([P, U, 8]),
                                        ALU.add))
                cf.link(V.tensor_reduce(g1[:, :, :], lg[:, :, :], AX.X, ALU.max))
                V.tensor_tensor(gd[:, :, :], lg[:, :, :], over8(g1[:, :, :]), ALU.subtract).then_inc(gate_in.sem, 1)
                ranks(cf, lg[:, :, :], 8, rk, req, rank)
                dve.wait_ge(gate_out.sem, gate_out.at(i, 1))
                cf.link(V.tensor_tensor(cw[:, :, :], ge[:, :, :], rank[:, :, :], ALU.mult))
                cf.link(V.tensor_reduce(g1[:, :, :], cw[:, :, :], AX.X, ALU.add))
                cf.link(V.reciprocal(g1[:, :, :], g1[:, :, :]))
                V.tensor_tensor(cw[:, :, :], cw[:, :, :], over8(g1[:, :, :]), ALU.mult).then_inc(cw_ready.sem, 1)
                dve.wait_ge(cwT_mm.sem, cwT_mm.at(i, 1))
                V.tensor_copy(cwT[:, :], D[0:8, 0:BT]).then_inc(cwT_ready.sem, 1)
                dve.wait_ge(b2_mm.sem, b2_mm.at(i, 1))
                dve.wait_ge(hx_ready.sem, hx_ready.at(i, 1))
                V.tensor_tensor(acc[:, :, :], two(C[:, 0:U * DIM]), acc[:, :, :], ALU.add).then_inc(acc0_ready.sem, 1)

            def add_expert(e, i):
                dve.wait_ge(y_mm.sem, y_mm.at(i, e + 1))
                if e == 0:
                    dve.wait_ge(acc0_ready.sem, acc0_ready.at(i, 1))
                else:
                    dve.wait_ge(y_taken.sem, y_taken.at(i, e))
                b = (D, C)[e % 2]
                for u in range(U):
                    ins = V.scalar_tensor_tensor(out=acc[:, u, :], in0=b[:, u * DIM:(u + 1) * DIM],
                                                 scalar=cw[:, u, e:e + 1], in1=acc[:, u, :],
                                                 op0=ALU.mult, op1=ALU.add)
                ins.then_inc(y_taken.sem, 1)

            def front_end(i):
                dve.wait_ge(y_taken.sem, y_taken.at(i, EXPERTS))
                if not first(i):
                    dve.wait_ge(h3_used.sem, h3_used.at(i, 0))
                norm(i, cf, acc, h3, 5, var_f, rstd_f, fb, h3_ready)
                cf.end()

            uc4 = uc.rearrange("p c (b n) -> p c b n", b=BI)

            def conv(i):
                cb.start(i)
                dve.wait_ge(xpad_ready.sem, xpad_ready.at(i, 1))
                last = [0] * CH
                for k in range(TAPS):
                    for c in range(CH):
                        if k:
                            cb.after(last[c])
                        src, w = xpad[:, c, :, k:k + SEQ], cols[:, c, k:k + 1]
                        if k == 0:
                            ins = V.tensor_scalar(uc4[:, c, :, :], src, w, None, ALU.mult)
                        else:
                            ins = V.scalar_tensor_tensor(out=uc4[:, c, :, :], in0=src, scalar=w, in1=uc4[:, c, :, :],
                                                         op0=ALU.mult, op1=ALU.add)
                        if (k, c) == (TAPS - 1, CH - 1):
                            ins.then_inc(uc_ready.sem, 1)
                        else:
                            last[c] = cb.step(ins)

            def bc(i):
                dve.wait_ge(bc_mm.sem, bc_mm.at(i, 1))
                src = two(Q[3][:, 0:64])
                cb.step(V.tensor_copy(bcf[:, :, STATE:], src[:, :, STATE:]))
                cb.link(V.tensor_reduce(bm[:, :, :], src[:, :, 0:STATE], AX.X, ALU.max))
                V.tensor_tensor(bd[:, :, :], src[:, :, 0:STATE], bm[:, :, :].broadcast_to([P, U, STATE]),
                                ALU.subtract).then_inc(bc_in.sem, 1)
                dve.wait_ge(bc_out.sem, bc_out.at(i, 1))
                cb.link(V.tensor_reduce(bm[:, :, :], be[:, :, :], AX.X, ALU.add))
                cb.link(V.reciprocal(bm[:, :, :], bm[:, :, :]))
                cb.link(V.tensor_tensor(bcf[:, :, 0:STATE], be[:, :, :], bm[:, :, :].broadcast_to([P, U, STATE]),
                                        ALU.mult))
                cb.link(V.tensor_copy(bc3[:, :, 0, :], bcf[:, :, :]))
                cb.link(V.tensor_tensor(bres[:, :, :], bcf[:, :, :], bc3[:, :, 0, :], ALU.subtract))
                cb.link(V.tensor_copy(bc3[:, :, 1, :], bres[:, :, :]))
                V.tensor_tensor(bc3[:, :, 2, :], bres[:, :, :], bc3[:, :, 1, :], ALU.subtract
                                ).then_inc(bc3_ready.sem, 1)

            def softplus(i):
                dve.wait_ge(sp_ready.sem, sp_ready.at(i, 1))
                V.tensor_tensor(delta[:, :, :], delta[:, :, :], dab[:, :, :], ALU.add).then_inc(delta_ready.sem, 1)

            def wide(ap):
                return ap.unsqueeze(1).broadcast_to([P, 2, BT])

            def flat2(ap):
                return ap.rearrange("p (k t) -> p k t", k=2)

            def scan_step(n, stage, i):
                sp2, c = divmod(n, CH)

                if stage == 0:
                    if n == 0:
                        dve.wait_ge(du_ready.sem, du_ready.at(i, 1))
                    if c == 0:
                        dve.wait_ge(bcast_mm.sem, bcast_mm.at(i, sp2 + 1))
                    if n >= SLOTS:
                        dve.wait_ge(y_added.sem, y_added.at(i, n - SLOTS + 1))
                    V.tensor_tensor(flat2(hs[n % SLOTS][:, :]), flat2(Q[sp2 % 2][:, :]), wide(du[:, c, :]),
                                    ALU.mult).then_inc(dbu_ready.sem, 1)
                elif stage == 1:
                    dve.wait_ge(dbu_ready.sem, dbu_ready.at(i, n + 1))
                    dve.wait_ge(dA_ready.sem, dA_ready.at(i, n + 1))
                    V.tensor_tensor_scan(hs[n % SLOTS][:, :], dA[n % 3][:, :, :].rearrange("p x n -> p (x n)"),
                                         hs[n % SLOTS][:, :], 0.0, ALU.mult, ALU.add
                                         ).then_inc(scan_ready.sem, 1)
                else:
                    dve.wait_ge(scan_ready.sem, scan_ready.at(i, n + 1))
                    V.tensor_tensor(hs[n % SLOTS][:, :], hs[n % SLOTS][:, :], Q[2 + sp2 % 2][:, :], ALU.mult
                                    ).then_inc(hc_ready.sem, 1)

            def scan_part(e, i):
                for n in range(CH * e, CH * e + CH):
                    scan_step(n, 0, i)
                    if n >= 1:
                        scan_step(n - 1, 1, i)
                    if n >= 2:
                        scan_step(n - 2, 2, i)
                if e == STATE // 2 - 1:
                    scan_step(STEPS - 1, 1, i)
                    scan_step(STEPS - 2, 2, i)
                    scan_step(STEPS - 1, 2, i)

            def after_scan(i):
                dve.wait_ge(out_mm.sem, out_mm.at(i, 1))
                V.tensor_tensor(rb[:, :, :], two(Q[0][:, 0:U * DIM]), h3[:, :, :], ALU.add).then_inc(h3_used.sem, 1)
                dve.wait_ge(h3_used.sem, h3_used.at(i, 1))
                norm(i, cb, rb, h4, 1, var_b, rstd_b, bb, h4_ready)

            def gate1(i):
                dve.wait_ge(th_ready.sem, th_ready.at(i, 1))
                cb.link(V.tensor_scalar(sc[:, :, :], th[:, :, :], 0.5, 0.5, ALU.mult, ALU.add))
                cb.link(V.tensor_tensor(sbias[:, :, :], sc[:, :, :], gate1_b.unsqueeze(1).broadcast_to([P, U, 8]),
                                        ALU.add))
                pairs = sbias[:, :, :].rearrange("p u (g k) -> p u g k", k=2)
                cb.link(V.tensor_tensor(gs[:, :, :], pairs[:, :, :, 0], pairs[:, :, :, 1], ALU.add))
                ranks(cb, gs[:, :, :], 4, b_rk, b_req, b_rank)
                cb.link(V.tensor_scalar(gr[:, :, :], b_rank[:, :, 0:4], 1.0, FAR, ALU.subtract, ALU.mult))
                cb.link(V.tensor_tensor(pairs, pairs, gr[:, :, :].unsqueeze(3).broadcast_to([P, U, 4, 2]), ALU.add))
                ranks(cb, sbias[:, :, :], 8, b_rk, b_req, b_rank)
                cb.link(V.tensor_tensor(cw2[:, :, :], sc[:, :, :], b_rank[:, :, :], ALU.mult))
                cb.link(V.tensor_reduce(b_g1[:, :, :], cw2[:, :, :], AX.X, ALU.add))
                cb.link(V.tensor_scalar(b_g1[:, :, :], b_g1[:, :, :], 1e-6, None, ALU.add))
                cb.link(V.reciprocal(b_g1[:, :, :], b_g1[:, :, :]))
                cb.link(V.tensor_tensor(cw2[:, :, :], cw2[:, :, :], over8(b_g1[:, :, :]), ALU.mult))

            def ffn_step(e, i):
                if e < FFN:
                    dve.wait_ge(sg_ready.sem, sg_ready.at(i, e + 1))
                    if e >= 2:
                        dve.wait_ge(fy_mm.sem, fy_mm.at(i, e - 1))
                    V.tensor_tensor(gg[e % 2][:, :], sg[e % 2][:, :], (Q[0], Q[3])[e % 2][:, BT:2 * BT], ALU.mult
                                    ).then_inc(gg_ready.sem, 1)
                if e:
                    p = e - 1
                    dve.wait_ge(fy_mm.sem, fy_mm.at(i, p + 1))
                    b = (Q[1], Q[2])[p % 2]
                    if p == 0:
                        V.tensor_tensor(rb[:, :, :], two(b[:, 0:U * DIM]), h4[:, :, :], ALU.add
                                        ).then_inc(fy_taken.sem, 1)
                    else:
                        dve.wait_ge(fy_taken.sem, fy_taken.at(i, p))
                        for u in range(U):
                            ins = V.scalar_tensor_tensor(out=rb[:, u, :], in0=b[:, u * DIM:(u + 1) * DIM],
                                                         scalar=cw2[:, u, p - 1:p], in1=rb[:, u, :],
                                                         op0=ALU.mult, op1=ALU.add)
                        ins.then_inc(fy_taken.sem, 1)

            def back_end(i):
                dve.wait_ge(fy_taken.sem, fy_taken.at(i, FFN))
                dve.wait_ge(fin_free.sem, fin_free.at(i, 16))
                norm(i, cb, rb, fin, 2, var_b, rstd_b, bb, fin_ready)
                cb.end()

            def step(i, b):
                if i is not None:
                    tok(i)
                    qk_l1(i)
                if b is not None:
                    conv(b)
                if i is not None:
                    linear_mask(i)
                if b is not None:
                    bc(b)
                if i is not None:
                    after_linear(i)
                if b is not None:
                    softplus(b)
                if i is not None:
                    softmax(i)
                    heads_out(i)
                    after_softmax(i)
                    gate(i)
                for e in range(EXPERTS):
                    if b is not None:
                        scan_part(e, b)
                    if i is not None:
                        add_expert(e, i)
                if b is not None:
                    after_scan(b)
                if i is not None:
                    front_end(i)
                if b is not None:
                    gate1(b)
                    for e in range(FFN + 1):
                        ffn_step(e, b)
                    back_end(b)

            step(0, None)
            with dve.Fori(1, BLOCKS) as i:
                step(i, i - 1)
            step(None, BLOCKS - 1)

        @block.gpsimd
        def _(pool):
            G = nc.gpsimd
            pool.wait_ge(ready.sem, 1)
            pool.wait_ge(ld["rows"].sem, 64)
            pool.wait_ge(ld["cst"].sem, 32)

            def power(var, rs, src, dst, k, i):
                pool.wait_ge(var.sem, var.at(i, k))
                G.tensor_tensor(dst[:, :], src[:, :], half_neg[:, :], ALU.pow).then_inc(rs.sem, 1)

            def add_bias(src, sig, k, row, dst, done, i):
                pool.wait_ge(sig.sem, sig.at(i, k))
                G.tensor_tensor(dst[:, :, :], src[:, :, :], row.unsqueeze(1).broadcast_to([P, U, DIM]), ALU.add
                                ).then_inc(done.sem, 1)

            def spread_keys(n, i):
                pool.wait_ge(k_ready.sem, k_ready.at(i, n + 1))
                G.tensor_tensor(kx[:, :, 0, :], kT[:, :, :],
                                cst[0:HALF, C_HEAD:C_HEAD + 1].unsqueeze(2).broadcast_to([HALF, 2, BT]), ALU.mult)
                for h in range(1, HH):
                    ins = G.tensor_scalar(kx[:, :, h, :], kT[:, :, :], cst[0:HALF, C_HEAD + h:C_HEAD + h + 1],
                                          None, ALU.mult)
                ins.then_inc(kx_ready.sem, 1)

            def sum_residuals(i):
                pool.wait_ge(xm_ready.sem, xm_ready.at(i, 1))
                G.tensor_tensor(acc[:, :, :], h1[:, :, :], xm[:, :, :], ALU.add).then_inc(hx_ready.sem, 1)

            def step_times_u(i):
                pool.wait_ge(delta_ready.sem, delta_ready.at(i, 1))
                pool.wait_ge(u_ready.sem, u_ready.at(i, 1))
                G.tensor_tensor(du[:, :, :], delta[:, :, :], uu[:, :, :], ALU.mult).then_inc(du_ready.sem, 1)

            def add_states(e, i):
                for c in range(CH):
                    n = e * CH + c
                    pool.wait_ge(hc_ready.sem, hc_ready.at(i, n + 1))
                    a, b = hs[n % SLOTS][:, 0:BT], hs[n % SLOTS][:, BT:2 * BT]
                    if e:
                        pool.wait_ge(y_added.sem, y_added.at(i, n - CH + 1))
                        G.tensor_tensor(a, a, b, ALU.add).then_inc(pair_added.sem, 1)
                        pool.wait_ge(pair_added.sem, pair_added.at(i, n - CH + 1))
                        G.tensor_tensor(yy[:, c, :], yy[:, c, :], a, ALU.add).then_inc(y_added.sem, 1)
                    else:
                        G.tensor_tensor(yy[:, c, :], a, b, ALU.add).then_inc(y_added.sem, 1)

            def gate_y(i):
                pool.wait_ge(y_added.sem, y_added.at(i, STEPS))
                pool.wait_ge(z_ready.sem, z_ready.at(i, 1))
                G.tensor_tensor(yy[:, :, :], yy[:, :, :], sz[:, :, :], ALU.mult).then_inc(yz_ready.sem, 1)

            def step(i, b):
                if i is not None:
                    power(var_f, rstd_f, ve, rstd, 1, i)
                    add_bias(h0, h_f, 1, proj1_b, hb, h0b_ready, i)
                    spread_keys(0, i)
                    power(var_f, rstd_f, ve, rstd, 2, i)
                    add_bias(h1, h1_ready, 1, proj2_b, hb, h1b_ready, i)
                if i is not None:
                    power(var_f, rstd_f, ve, rstd, 3, i)
                if b is not None:
                    step_times_u(b)
                if i is not None:
                    spread_keys(1, i)
                    power(var_f, rstd_f, ve, rstd, 4, i)
                    sum_residuals(i)
                if b is not None:
                    for e in range(STATE // 2):
                        add_states(e, b)
                    gate_y(b)
                    power(var_b, rstd_b, veb, rstdb, 1, b)
                if i is not None:
                    power(var_f, rstd_f, ve, rstd, 5, i)
                if b is not None:
                    power(var_b, rstd_b, veb, rstdb, 2, b)

            step(0, None)
            with pool.Fori(1, BLOCKS) as i:
                step(i, i - 1)
            step(None, BLOCKS - 1)

def laid_out(x, weights):
    import numpy as np

    def halves(w):
        return w.reshape(2, HALF, -1).transpose(1, 0, 2)

    def chunks(w, k):
        return w.reshape(k, P, -1).transpose(1, 0, 2)

    w = weights
    own = [(c, r, q) for c in range(CHANNELS) for r in range(PATCH) for q in range(PATCH)]
    ring = [(c, r, q) for c in range(CHANNELS) for r in (-1, PATCH) for q in range(PATCH)]
    ring += [(c, r, q) for c in range(CHANNELS) for r in range(PATCH) for q in (-1, PATCH)]
    pc, pr, pq = np.array(own + ring).T
    padded = np.pad(x, ((0, 0), (0, 0), (1, 1), (1, 1)))
    g = SIDE // PATCH
    ty, tx = np.divmod(np.arange(g * g), g)
    px = padded[:, pc[:, None], pr[:, None] + 1 + PATCH * ty, pq[:, None] + 1 + PATCH * tx]
    px = px.reshape(BLOCKS, BI, PK, PR, SEQ).transpose(0, 3, 2, 1, 4).reshape(BLOCKS, PR, PK * BT)
    rows = np.full((SHIFTS, PIXELS), PATCH_DIM)
    for s, (dr, dq) in enumerate(((0, 0), (0, 1), (0, -1), (1, 0), (-1, 0))):
        r, q = pr + dr, pq + dq
        ok = (r >= 0) & (r < PATCH) & (q >= 0) & (q < PATCH)
        rows[s, ok] = ((r * PATCH + q) * 5 * CHANNELS + s * CHANNELS + pc)[ok]
    at = rows.reshape(SHIFTS, PK, PR).transpose(2, 0, 1)

    def patch(v):
        return np.pad(v, ((0, 1),) + ((0, 0),) * (v.ndim - 1))[at]

    cst = np.zeros((P, C_END), np.float32)
    p = np.arange(P)[:, None]
    cst[:, C_IDENT:C_IDENT + P] = np.eye(P)
    same = (p % 32) // SEQ == np.arange(32) // SEQ
    cst[:, C_MASK:C_MASK + 32] = same
    cst[:, C_NEG:C_NEG + 32] = np.where(same, 0.0, -FAR)
    cst[:, C_HEAD:C_HEAD + HH] = p // HD == np.arange(HH)
    cst[:, C_TRI:C_TRI + 64] = (np.arange(8) < np.arange(8)[:, None]).reshape(1, 64)
    cst[0:PR, C_CNT:C_CNT + PK] = (at < PATCH_DIM).sum(1)
    cols = np.concatenate([w["L1_attn_conv_w"].reshape(INNER, TAPS), w["L1_attn_conv_b"][:, None],
                           w["L1_attn_b_dt"][:, None], w["L1_attn_A_log"]], 1)
    ln12 = np.concatenate([w["L0_ffn_" + n].reshape(2, HALF).T for n in ("ln1_g", "ln1_b", "ln2_g", "ln2_b")], 1)

    def stacked(routed, shared):
        return np.concatenate([shared[None], routed])

    f1, f3, f2 = (stacked(w["L1_ffn_w" + n], w["L1_ffn_sw" + n]) for n in "132")
    return {
        "x": px, "cst": cst,
        "tokgb": np.stack([patch(w["L0_tok_ln_gamma"]), patch(w["L0_tok_ln_beta"])], 1),
        "tok_w": patch(w["L0_tok_w"]),
        "rows": np.concatenate([w["L0_tok_b"], w["L0_attn_b_proj"], w["L0_ffn_proj_b"], w["L0_ffn_gate_b"],
                                w["L1_ffn_gate_bias"]]),
        "ln12": ln12, "cols": chunks(cols, CH),
        "qkv1": halves(w["L0_attn_w_qkv"].T), "proj1": halves(w["L0_attn_w_proj"].T),
        "qkv2": halves(w["L0_ffn_qkv_w"]), "proj2": halves(w["L0_ffn_proj_w"]),
        "gate0": halves(w["L0_ffn_gate_w"]), "b2": w["L0_ffn_b2"],
        "b1": w["L0_ffn_b1"].reshape(EXPERTS * HM, P).T,
        "w1": w["L0_ffn_w1"].reshape(EXPERTS, 2, HALF, HIDDEN).transpose(0, 2, 1, 3),
        "w2": w["L0_ffn_w2"].reshape(EXPERTS, HM, P, DIM).transpose(0, 2, 1, 3),
        "in_w": halves(w["L1_attn_W_in"]), "x_w": chunks(w["L1_attn_W_x"], CH),
        "dt_w": chunks(w["L1_attn_W_dt"], CH), "out_w": chunks(w["L1_attn_W_out"], CH),
        "gate1": halves(w["L1_ffn_gate_weight"].T),
        "f1": halves(f1.reshape(FFN * INTER, DIM).T), "f3": halves(f3.reshape(FFN * INTER, DIM).T),
        "f2": f2.transpose(2, 0, 1),
    }

def kernel(**inputs):
    import numpy as np
    import concourse.bacc as bacc
    from concourse.bass_utils import run_bass_kernel_spmd

    nc = bacc.Bacc("TRN2", target_bir_lowering=False, num_devices=1,
                   dynamic_dma_scratch_size=1024)
    host = {k: np.asarray(v) for k, v in inputs.items()}
    arrays, aps = {}, {}
    for name, a in laid_out(host["x"], host).items():
        a = np.ascontiguousarray(a)
        arrays[f"in_{name}"] = a
        aps[name] = nc.dram_tensor(f"in_{name}", a.shape, mybir.dt.from_np(a.dtype), kind="ExternalInput").ap()
    out = nc.dram_tensor("out", (BLOCKS, U, P, DIM), F32, kind="ExternalOutput").ap()
    tower(nc, aps, out)
    r = run_bass_kernel_spmd(nc, [arrays], core_ids=[0])
    return r.results[0]["out"].reshape(IMAGES, SEQ, DIM)
```

```python
import concourse.bass as bass
from concourse import mybir
from contextlib import ExitStack

F32 = mybir.dt.float32
BF16 = mybir.dt.bfloat16
F32R = mybir.dt.float32r
ALU = mybir.AluOpType
ACT = mybir.ActivationFunctionType
AX = mybir.AxisListType

IMAGES, CHANNELS, SIDE, PATCH = 64, 3, 64, 16
SEQ = (SIDE // PATCH) ** 2
TOKENS = IMAGES * SEQ
DIM, HEADS = 192, 12
HD = DIM // HEADS
HALF = DIM // 2
HH = HEADS // 2
P = 128
BT = 256
U = BT // P
BLOCKS = TOKENS // BT
BI = BT // SEQ
PATCH_DIM = PATCH * PATCH * 5 * CHANNELS
SHIFTS = 5
PIXELS = CHANNELS * (PATCH * PATCH + 4 * PATCH)
PR = 120
PK = PIXELS // PR
EXPERTS, HIDDEN = 8, 768
HM = HIDDEN // P
UNITS = EXPERTS * HM // 2
REST = DIM - P
INNER, STATE, TAPS = 384, 16, 4
CH = INNER // P
INTER = 128
FFN = EXPERTS + 1
EPS = 1e-5
FAR = 1e30

C_IDENT = 0
C_MASK = C_IDENT + P
C_NEG = C_MASK + 32
C_HEAD = C_NEG + 32
C_TRI = C_HEAD + HH
C_CNT = C_TRI + 64
C_END = C_CNT + PK

def first(i):
    return isinstance(i, int) and i == 0

class Signal:

    def __init__(self, sem, per):
        self.sem, self.per = sem, per

    def at(self, i, k):
        return i * self.per + k

class Chain:

    def __init__(self, eng, sig):
        self.eng, self.sig, self.i, self.n = eng, sig, 0, 0

    def start(self, i):
        self.i, self.n = i, 0

    def end(self):
        assert self.n == self.sig.per, (self.n, self.sig.per)

    def step(self, ins):
        self.n += 1
        ins.then_inc(self.sig.sem, 1)
        return self.n

    def after(self, n):
        self.eng.wait_ge(self.sig.sem, self.sig.at(self.i, n))

    def link(self, ins):
        self.after(self.step(ins))

def tower(nc, d, out):
    ctx = ExitStack()
    with ctx:
        def sb(name, shape, dt=F32):
            return ctx.enter_context(nc.sbuf_tensor(name, shape, dt))

        def bank(name):
            return ctx.enter_context(nc.psum_tensor(name, [P, 512], F32))

        def signal(name, per=1):
            return Signal(ctx.enter_context(nc.semaphore(name)), per)

        cst = sb("cst", [P, C_END])
        ident = cst[:, C_IDENT:C_IDENT + P]
        mask = cst[:, C_MASK:C_MASK + 32]
        neg = cst[:, C_NEG:C_NEG + 32]
        tri = cst[:, C_TRI:C_TRI + 64].rearrange("p (e f) -> p e f", e=8)
        cnt = cst[0:PR, C_CNT:C_CNT + PK]
        rows = sb("rows", [P, 3 * DIM + 16])
        tok_b, proj1_b, proj2_b = (rows[:, n * DIM:(n + 1) * DIM] for n in range(3))
        gate0_b, gate1_b = rows[:, 3 * DIM:3 * DIM + 8], rows[:, 3 * DIM + 8:3 * DIM + 16]
        ln1_gb = sb("ln1_gb", [HALF, 4])
        tokgb = sb("tokgb", [PR, 2, SHIFTS, PK])
        qkv_w = [sb(f"qkv_w{n}", [HALF, 2, 3 * DIM]) for n in range(2)]
        proj_w = [sb(f"proj_w{n}", [HALF, 2, DIM]) for n in range(2)]
        gate0_w = sb("gate0_w", [P, 2, EXPERTS])
        w1_raw = sb("w1_raw", [P, 2, HIDDEN])
        RING = 3
        w1_hi = [sb(f"w1_hi{n}", [P, 2, 2 * P], F32R) for n in range(RING)]
        w1_lo = [sb(f"w1_lo{n}", [P, 2, 2 * P], F32R) for n in range(RING)]
        b1 = sb("b1", [P, EXPERTS * HM])
        w2 = [sb(f"w2_{n}", [P, HM, DIM]) for n in range(2)]
        b2 = sb("b2", [EXPERTS, DIM])
        in_w = sb("in_w", [HALF, 2, 2 * INNER])
        cols = sb("cols", [P, CH, TAPS + 2 + STATE])
        x_w = sb("x_w", [P, CH, 2 * STATE + INNER])
        dt_w = sb("dt_w", [P, CH, INNER])
        out_w = sb("out_w", [P, CH, DIM])
        gate1_w = sb("gate1_w", [HALF, 2, EXPERTS])
        f1_w = sb("f1_w", [HALF, 2, FFN * INTER])
        f3_w = sb("f3_w", [HALF, 2, FFN * INTER])
        f2_w = sb("f2_w", [INTER, FFN, DIM])

        tokw = sb("tokw", [PR, PK, DIM + 1])
        tok_cs = sb("tok_cs", [P, DIM])
        tok_bw = sb("tok_bw", [P, DIM])
        ones = sb("ones", [P, P])
        idle = sb("idle", [P, 1])
        half_neg = sb("half_neg", [P, U])
        identb = sb("identb", [P, P], BF16)
        pick = sb("pick", [HALF, 32], BF16)
        decay = sb("decay", [P, CH, STATE])

        xb = sb("xb", [PR, PK, BT])
        shared = sb("shared", [P, 2 * HH * BT])
        sq = shared[0:PR, 0:PK * BT].rearrange("p (k t) -> p k t", k=PK)
        kx = shared[0:HALF, :].rearrange("p (m h t) -> p m h t", m=2, h=HH)
        st = sb("st", [P, U, 6])
        mv = sb("mv", [P, U, 2])
        ve = sb("ve", [P, U])
        rstd = sb("rstd", [P, U])
        stm, mvm, vem, rstdm = (sb(n, s) for n, s in (("stm", [P, U, 6]), ("mvm", [P, U, 2]), ("vem", [P, U]),
                                                      ("rstdm", [P, U])))
        he = [sb(f"he{n}", [P, HM, BT]) for n in range(2)]
        tmp = sb("tmp", [P, U, DIM])
        h0, hb, h1, acc = (sb(n, [P, U, DIM]) for n in ("h0", "hb", "h1", "acc"))
        z = sb("z", [P, U, DIM + REST])
        xm = h0
        hT = sb("hT", [HALF, 2, BT])
        qT = sb("qT", [HALF, 2, BT])
        kT = sb("kT", [HALF, 2, BT])
        vx = sb("vx", [P, U, HEADS, 2 * HD])
        l1 = sb("l1", [HALF, 2, 2 * BI])
        pm = sb("pm", [P, U, HEADS, 32])
        pbd = sb("pbd", [P, U * HEADS, P])
        mx = sb("mx", [P, U * HEADS])
        oT = sb("oT", [HALF, 2, BT])
        h2T = sb("h2T", [P, 2, BT])
        h2_hi = sb("h2_hi", [P, BT], F32R)
        h2_lo = sb("h2_lo", [P, BT], F32R)
        h2_rest = sb("h2_rest", [P, BT], F32R)
        ln2_gb = sb("ln2_gb", [P, 4])
        lg = sb("lg", [P, U, 8])
        rk = sb("rk", [P, U, 8, 8])
        req = sb("req", [P, U, 8, 8])
        rank = sb("rank", [P, U, 8])
        g1 = sb("g1", [P, U, 1])
        gd = sb("gd", [P, U, 8])
        ge = sb("ge", [P, U, 8])
        cw = sb("cw", [P, U, 8])
        cwT = sb("cwT", [EXPERTS, BT])

        h3 = sb("h3", [P, U, DIM])
        h3T = sb("h3T", [HALF, 2, BT])
        h4T = sb("h4T", [HALF, 2, BT])
        LONG = CH * BT
        RAW = SHIFTS * PK * DIM
        long = sb("long", [P, RAW])
        at = [0]

        def part(n):
            at[0] += n
            return long[:, at[0] - n:at[0]]

        uc, sz, uu, dtp, delta, yy = (part(LONG).rearrange("p (c t) -> p c t", c=CH) for _ in range(6))
        dab, du = uc, dtp
        SLOTS = 4
        hs = [part(2 * BT) for _ in range(SLOTS)]
        h4, rb = (part(U * DIM).rearrange("p (u e) -> p u e", u=U) for _ in range(2))
        spare = part(BT)
        wraw = long[0:PR, :].rearrange("p (s k e) -> p s k e", s=SHIFTS, k=PK)
        xpad = sb("xpad", [P, CH, BI, SEQ + TAPS - 1])
        bm = sb("bm", [P, U, 1])
        bd = sb("bd", [P, U, STATE])
        be = sb("be", [P, U, STATE])
        bcf = sb("bcf", [P, U, 2 * STATE])
        bres = sb("bres", [P, U, 2 * STATE])
        bc3 = sb("bc3", [P, U, 3, 2 * STATE], BF16)
        bcT = sb("bcT", [HALF, BT], BF16)
        dA = [sb(f"dA{n}", [P, 2 * BI, SEQ]) for n in range(3)]
        stb = sb("stb", [P, U, 6])
        mvb = sb("mvb", [P, U, 2])
        veb = sb("veb", [P, U])
        rstdb = sb("rstdb", [P, U])
        fin = sb("fin", [P, U, DIM])
        th = sb("th", [P, U, 8])
        sc = sb("sc", [P, U, 8])
        sbias = sb("sbias", [P, U, 8])
        gs = sb("gs", [P, U, 4])
        gr = sb("gr", [P, U, 4])
        cw2 = sb("cw2", [P, U, 8])
        b_rk, b_req = rk, req
        b_rank = sb("b_rank", [P, U, 8])
        b_g1 = sb("b_g1", [P, U, 1])
        sg = [sb(f"sg{n}", [P, BT]) for n in range(2)]
        gg = [sb("gg0", [P, BT]), spare]

        H0, H1 = (bank(f"hidden{n}") for n in range(2))
        Y = bank("outs")
        X0, X1 = (bank(f"attn{n}") for n in range(2))
        R = [bank(f"ring{n}") for n in range(3)]

        loads = ["cst", *(f"tok{n}" for n in range(SHIFTS)), "rows", "attn1", "attn2", "gate0", "scan", "ffn"]
        ld = {n: signal("loaded_" + n) for n in loads}
        x_loaded = signal("x_loaded", 16)
        w1_loaded = signal("w1_loaded", 16 * EXPERTS)
        w2_loaded = [signal(f"w2_loaded{n}", 16 * EXPERTS // 2) for n in range(2)]
        ready = signal("constants_ready")
        beta_mm, tokw_ready, colsum_mm = signal("beta_mm"), signal("tokw_ready"), signal("colsum_mm")
        tok_mm = signal("tok_mm", 2)
        sq_ready = signal("sq_ready")
        var_a, rstd_a = signal("var_a", 4), signal("rstd_a", 4)
        h_a = signal("h_a", 3)
        t_a = signal("t_a", 2)
        tc_a = signal("tc_a", 4)
        h0b_ready, h1_ready, h1b_ready = signal("h0b_ready"), signal("h1_ready"), signal("h1b_ready")
        xm_ready = signal("xm_ready")
        qk_mm, v_mm = signal("qk_mm", 2), signal("v_mm", 2)
        q_ready = signal("q_ready", 2)
        k_ready = signal("k_ready", 2)
        kx_ready, v_ready = signal("kx_ready", 2), signal("v_ready", 2)
        s_mm = signal("s_mm", 2)
        sm_in, sm_out = signal("sm_in"), signal("sm_out")
        pbd_ready, pv_mm = signal("pbd_ready", 2), signal("pv_mm", 2)
        proj_mm = signal("proj_mm", 2)
        t_z2, h2T_ready, hx_ready = signal("t_z2"), signal("h2T_ready"), signal("hx_ready")
        gate_mm, gate_in, gate_out = signal("gate_mm"), signal("gate_in"), signal("gate_out")
        cw_ready, cwT_mm, cwT_ready, b2_mm = (signal("cw_ready"), signal("cwT_mm"), signal("cwT_ready"),
                                              signal("b2_mm"))
        acc0_ready = signal("acc0_ready")
        hid_mm, hid_ready = signal("hid_mm", EXPERTS * HM // 2), signal("hid_ready", EXPERTS * HM // 2)
        y_mm, y_taken = signal("y_mm", EXPERTS), signal("y_taken", EXPERTS)
        w1_rounded, w1_ready = signal("w1_rounded", UNITS), signal("w1_ready", UNITS)
        h2_rounded, h2_ready = signal("h2_rounded"), signal("h2_ready")
        var_m, rstd_m = signal("var_m"), signal("rstd_m")
        h3_ready = signal("h3_ready")
        t_h3, h3T_ready = signal("t_h3"), signal("h3T_ready")
        xz_mm, xpad_ready, z_ready = signal("xz_mm", 2), signal("xpad_ready"), signal("z_ready")
        uc_ready, u_ready = signal("uc_ready"), signal("u_ready")
        bc_mm, bc_in, bc_out, bc3_ready = signal("bc_mm"), signal("bc_in"), signal("bc_out"), signal("bc3_ready")
        dtp_mm, dtp_ready, dt_mm = signal("dtp_mm"), signal("dtp_ready"), signal("dt_mm")
        abs_done, exp_done, sp_ready = signal("abs_done"), signal("exp_done"), signal("sp_ready")
        t_bc, bcT_ready = signal("t_bc"), signal("bcT_ready")
        delta_ready, du_ready = signal("delta_ready"), signal("du_ready")
        STEPS = STATE // 2 * CH
        bcast_mm = signal("bcast_mm", STATE)
        dA_ready, dbu_ready, scan_ready, hc_ready, y_added = (signal(n, STEPS) for n in (
            "dA_ready", "dbu_ready", "scan_ready", "hc_ready", "y_added"))
        pair_added = signal("pair_added", STEPS - CH)
        yz_ready, out_mm, scanned = signal("yz_ready", CH), signal("out_mm"), signal("scanned")
        kept = signal("kept")
        var_b, rstd_b = signal("var_b", 2), signal("rstd_b", 2)
        h4_ready, t_h4, h4T_ready = signal("h4_ready"), signal("t_h4"), signal("h4T_ready")
        gate1_mm, th_ready = signal("gate1_mm"), signal("th_ready")
        f13_mm, sg_ready, gg_ready, fy_mm, fy_taken = (signal(n, FFN) for n in (
            "f13_mm", "sg_ready", "gg_ready", "fy_mm", "fy_taken"))
        fin_ready, fin_free = signal("fin_ready"), signal("fin_free", 16)
        exp_a, neg_a, tokw_part = signal("exp_a"), signal("neg_a"), signal("tokw_part")
        dve_a, dve_m, dve_s, dve_b = (signal("dve_a", 30), signal("dve_m", 15), signal("dve_s", 19),
                                      signal("dve_b", 30))

        block = ctx.enter_context(nc.Block())

        @block.sync
        def _(sp):
            def load(name, *pairs):
                for dst, src in pairs:
                    sp.dma_start(dst, src).then_inc(ld[name].sem, 16)

            def load_x(i):
                sp.dma_start(xb[:, :, :].rearrange("p k t -> p (k t)"),
                             d["x"][bass.ds(i, 1), :, :].rearrange("a p n -> (a p) n")
                             ).then_inc(x_loaded.sem, 16)

            def store(b):
                sp.wait_ge(fin_ready.sem, fin_ready.at(b, 1))
                sp.dma_start(out[bass.ds(b, 1), :, :, :].rearrange("a u p e -> (a p) u e"), fin[:, :, :]
                              ).then_inc(fin_free.sem, 16)

            def next_pixels(i):
                sp.wait_ge(tok_mm.sem, tok_mm.at(i, 2))
                load_x(i + 1)

            def load_experts(i):
                for e in range(EXPERTS + 1):
                    if e < EXPERTS:
                        if e >= 1:
                            sp.wait_ge(w1_ready.sem, w1_ready.at(i, e * HM // 2))
                        elif not first(i):
                            sp.wait_ge(w1_ready.sem, w1_ready.at(i, 0))
                        sp.dma_start(w1_raw[:, :, :], d["w1"][e, :, :, :]).then_inc(w1_loaded.sem, 16)
                    if e:
                        p = e - 1
                        if p >= 2:
                            sp.wait_ge(y_mm.sem, y_mm.at(i, p - 1))
                        elif not first(i):
                            sp.wait_ge(y_mm.sem, y_mm.at(i, 0))
                        sp.dma_start(w2[p % 2][:, :, :], d["w2"][p, :, :, :]).then_inc(w2_loaded[p % 2].sem, 16)

            sp.sem_inc(fin_free.sem, 16)
            load("cst", (cst[:, :], d["cst"]), (tokgb[:, :, :, :], d["tokgb"]))
            for s in range(SHIFTS):
                load(f"tok{s}", (wraw[:, s, :, :], d["tok_w"][:, s, :, :]))
            load_x(0)
            load("rows", (rows[:, :], d["rows"].partition_broadcast(P)), (ln1_gb[:, :], d["ln1_gb"]),
                 (cols[:, :, :], d["cols"]), (b1[:, :], d["b1"]))
            load("attn1", (qkv_w[0][:, :, :], d["qkv1"]), (proj_w[0][:, :, :], d["proj1"]))
            load("attn2", (qkv_w[1][:, :, :], d["qkv2"]), (proj_w[1][:, :, :], d["proj2"]))
            load("gate0", (gate0_w[:, :, :], d["gate0"]), (b2[:, :], d["b2"]), (ln2_gb[:, :], d["ln2_gb"]))
            load("scan", (in_w[:, :, :], d["in_w"]), (x_w[:, :, :], d["x_w"]),
                 (dt_w[:, :, :], d["dt_w"]), (out_w[:, :, :], d["out_w"]))
            load("ffn", (gate1_w[:, :, :], d["gate1"]), (f1_w[:, :, :], d["f1"]), (f3_w[:, :, :], d["f3"]),
                 (f2_w[:, :, :], d["f2"]))
            sp.wait_ge(tok_mm.sem, tok_mm.at(0, 2))
            load_x(1)
            load_experts(0)
            next_pixels(1)
            load_experts(1)
            with sp.Fori(2, BLOCKS - 1) as i:
                next_pixels(i)
                load_experts(i)
                store(i - 2)
            load_experts(BLOCKS - 1)
            for b in range(BLOCKS - 3, BLOCKS):
                store(b)
            sp.wait_ge(fin_free.sem, fin_free.at(BLOCKS, 16))

        @block.tensor
        def _(pe):
            def mm(o, l, r, first=True, last=True):
                return nc.tensor.matmul(o, l, r, start=first, stop=last)

            def turn(src, dst, sig):
                for h in range(2):
                    for u in range(U):
                        ins = nc.tensor.transpose(dst[0:HALF, h * BT + u * P:h * BT + (u + 1) * P],
                                                  src[:, u, h * HALF:(h + 1) * HALF], ident)
                ins.then_inc(sig.sem, 1)

            def loaded(name, n):
                pe.wait_ge(ld[name].sem, 16 * n)

            loaded("cst", 2)
            for s in range(SHIFTS):
                loaded(f"tok{s}", 1)
                for k in range(PK):
                    ins = mm(H0[:, 0:DIM], tokgb[:, 1, s, k:k + 1].broadcast_to([PR, P]), wraw[:, s, k, :],
                             s == 0 and k == 0, s == SHIFTS - 1 and k == PK - 1)
            ins.then_inc(beta_mm.sem, 1)
            pe.wait_ge(ready.sem, 1)
            pe.wait_ge(tokw_ready.sem, 1)
            for k in range(PK):
                ins = mm(H1[:, 0:DIM], ones[0:PR, :], tokw[:, k, 0:DIM], k == 0, k == PK - 1)
            ins.then_inc(colsum_mm.sem, 1)
            for name, n in (("attn1", 2), ("attn2", 2)):
                loaded(name, n)

            def tok(a):
                pe.wait_ge(x_loaded.sem, x_loaded.at(a, 16))
                for u in range(U):
                    for k in range(PK):
                        ins = mm(X0[:, u * (DIM + 1):(u + 1) * (DIM + 1)], xb[:, k, u * P:(u + 1) * P],
                                 tokw[:, k, :], k == 0, k == PK - 1)
                ins.then_inc(tok_mm.sem, 1)

            def tok_squares(a):
                pe.wait_ge(sq_ready.sem, sq_ready.at(a, 1))
                for u in range(U):
                    for k in range(PK):
                        at = U * (DIM + 1) + u
                        ins = mm(X0[:, at:at + 1], sq[:, k, u * P:(u + 1) * P], cnt[:, k:k + 1],
                                 k == 0, k == PK - 1)
                ins.then_inc(tok_mm.sem, 1)

            def turn_input(n, a):
                pe.wait_ge(h_a.sem, h_a.at(a, n + 1))
                turn((h0, z)[n], X1, t_a)

            def queries_keys(n, a):
                pe.wait_ge(tc_a.sem, tc_a.at(a, 2 * n + 1))
                for part, bank_ in ((0, X0), (1, X1)):
                    for m in range(2):
                        at = part * DIM + m * HALF
                        for kk in range(2):
                            ins = mm(bank_[0:HALF, m * BT:(m + 1) * BT], qkv_w[n][:, kk, at:at + HALF],
                                     hT[:, kk, :], kk == 0, kk == 1)
                ins.then_inc(qk_mm.sem, 1)

            def values(n, a):
                pe.wait_ge(q_ready.sem, q_ready.at(a, n + 1))
                for u in range(U):
                    for kk in range(2):
                        ins = mm(X0[:, u * DIM:(u + 1) * DIM], hT[:, kk, u * P:(u + 1) * P],
                                 qkv_w[n][:, kk, 2 * DIM:3 * DIM], kk == 0, kk == 1)
                ins.then_inc(v_mm.sem, 1)

            def scores(n, a):
                pe.wait_ge(kx_ready.sem, kx_ready.at(a, n + 1))
                pe.wait_ge(v_ready.sem, v_ready.at(a, n + 1))
                for u, bank_ in ((0, X0), (1, X1)):
                    for g in range(4):
                        at = u * P + 32 * g
                        for m in range(2):
                            ins = mm(bank_[32 * g:32 * g + 32, m * HH * 32:(m + 1) * HH * 32],
                                     qT[:, m, at:at + 32], kx[:, m, :, at:at + 32])
                ins.then_inc(s_mm.sem, 1)

            def weigh_values(n, a):
                pe.wait_ge(pbd_ready.sem, pbd_ready.at(a, n + 1))
                for u in range(U):
                    for h in range(HEADS):
                        half, pair, k = h // HH, h % HH // 2, h % 2
                        at = half * BT + u * P
                        ins = mm(X1[32 * pair:32 * pair + 32, at:at + P], vx[:, u, h, :],
                                 pbd[:, u * HEADS + h, :], k == 0, k == 1)
                ins.then_inc(pv_mm.sem, 1)

            def project(n, a):
                pe.wait_ge(tc_a.sem, tc_a.at(a, 2 * n + 2))
                for u in range(U):
                    for kk in range(2):
                        ins = mm(X0[:, u * DIM:(u + 1) * DIM], oT[:, kk, u * P:(u + 1) * P],
                                 proj_w[n][:, kk, :], kk == 0, kk == 1)
                ins.then_inc(proj_mm.sem, 1)

            def turn_z2(m):
                if first(m):
                    loaded("gate0", 3)
                else:
                    pe.wait_ge(bcT_ready.sem, bcT_ready.at(m, 0))
                pe.wait_ge(h_a.sem, h_a.at(m, 3))
                for u in range(U):
                    nc.tensor.transpose(Y[:, u * P:(u + 1) * P], z[:, u, 0:P], ident)
                    ins = nc.tensor.transpose(Y[:, BT + u * P:BT + (u + 1) * P],
                                              z[:, u, P:2 * P], ident)
                ins.then_inc(t_z2.sem, 1)

            def gate(m):
                pe.wait_ge(h2T_ready.sem, h2T_ready.at(m, 1))
                for u in range(U):
                    for kk, k in ((0, P), (1, REST)):
                        ins = mm(Y[:, u * 8:u * 8 + 8], h2T[0:k, kk, u * P:(u + 1) * P], gate0_w[0:k, kk, :],
                                 kk == 0, kk == 1)
                ins.then_inc(gate_mm.sem, 1)

            def gate_bias(m):
                pe.wait_ge(cw_ready.sem, cw_ready.at(m, 1))
                for u in range(U):
                    ins = nc.tensor.transpose(Y[0:8, u * P:(u + 1) * P], cw[:, u, :], ident)
                ins.then_inc(cwT_mm.sem, 1)
                pe.wait_ge(cwT_ready.sem, cwT_ready.at(m, 1))
                for u in range(U):
                    ins = mm(Y[:, u * DIM:(u + 1) * DIM], cwT[:, u * P:(u + 1) * P], b2[:, :])
                ins.then_inc(b2_mm.sem, 1)

            def hidden(e, m):
                if e == 0:
                    pe.wait_ge(h2_ready.sem, h2_ready.at(m, 1))
                for mp in range(HM // 2):
                    unit = e * HM // 2 + mp
                    pe.wait_ge(w1_ready.sem, w1_ready.at(m, unit + 1))
                    if unit >= 2:
                        pe.wait_ge(hid_ready.sem, hid_ready.at(m, unit - 1))
                    hi, lo = w1_hi[unit % RING], w1_lo[unit % RING]
                    for k in range(2):
                        o, c = (H0, H1)[unit % 2][:, k * BT:(k + 1) * BT], slice(k * P, (k + 1) * P)
                        mm(o, hi[:, 0, c], h2_hi[:, :], True, False)
                        mm(o, hi[:, 0, c], h2_lo[:, :], False, False)
                        mm(o, lo[:, 0, c], h2_hi[:, :], False, False)
                        mm(o, hi[:, 1, c], h2_rest[:, :], False, False)
                        ins = mm(o, lo[0:REST, 1, c], h2_rest[0:REST, :], False, True)
                    ins.then_inc(hid_mm.sem, 1)

            def expert_out(e, m):
                pe.wait_ge(w2_loaded[e % 2].sem, w2_loaded[e % 2].at(m, 16 * (e // 2 + 1)))
                pe.wait_ge(hid_ready.sem, hid_ready.at(m, (e + 1) * HM // 2))
                if e == 0:
                    pe.wait_ge(acc0_ready.sem, acc0_ready.at(m, 1))
                elif e < EXPERTS - 1:
                    pe.wait_ge(y_taken.sem, y_taken.at(m, e))
                y = H0 if e == EXPERTS - 1 else Y
                for u in range(U):
                    for k in range(HM):
                        ins = mm(y[:, u * DIM:(u + 1) * DIM], he[e % 2][:, k, u * P:(u + 1) * P],
                                 w2[e % 2][:, k, :], k == 0, k == HM - 1)
                ins.then_inc(y_mm.sem, 1)

            def turn_h3(m):
                pe.wait_ge(h3_ready.sem, h3_ready.at(m, 1))
                turn(h3, H1, t_h3)

            def xz(m):
                if first(m):
                    loaded("scan", 4)
                    loaded("ffn", 4)
                pe.wait_ge(h3T_ready.sem, h3T_ready.at(m, 1))
                for k in range(2 * CH):
                    for kk in range(2):
                        ins = mm((H0, H1, Y)[k // 2][:, (k % 2) * BT:(k % 2 + 1) * BT],
                                 in_w[:, kk, k * P:(k + 1) * P], h3T[:, kk, :], kk == 0, kk == 1)
                    if k == CH - 1:
                        ins.then_inc(xz_mm.sem, 1)
                ins.then_inc(xz_mm.sem, 1)

            def bc_dt(m):
                pe.wait_ge(u_ready.sem, u_ready.at(m, 1))
                for u in range(U):
                    for c in range(CH):
                        ins = mm(Y[:, u * 32:(u + 1) * 32], uu[:, c, u * P:(u + 1) * P],
                                 x_w[:, c, 0:32], c == 0, c == CH - 1)
                ins.then_inc(bc_mm.sem, 1)
                for k in range(CH):
                    for c in range(CH):
                        ins = mm((H0, H1)[k // 2][:, (k % 2) * BT:(k % 2 + 1) * BT],
                                 x_w[:, c, 32 + k * P:32 + (k + 1) * P], uu[:, c, :], c == 0, c == CH - 1)
                ins.then_inc(dtp_mm.sem, 1)

            def dt(m):
                pe.wait_ge(dtp_ready.sem, dtp_ready.at(m, 1))
                for k in range(CH):
                    for c in range(CH):
                        ins = mm((X0, X1)[k // 2][:, (k % 2) * BT:(k % 2 + 1) * BT],
                                 dt_w[:, c, k * P:(k + 1) * P], dtp[:, c, :], c == 0, c == CH - 1)
                ins.then_inc(dt_mm.sem, 1)

            def turn_bc(m):
                pe.wait_ge(bc3_ready.sem, bc3_ready.at(m, 1))
                for u in range(U):
                    ins = nc.tensor.transpose(Yb[0:HALF, u * P:(u + 1) * P],
                                              bc3[:, u, :, :].rearrange("p a s -> p (a s)"), identb[:, :])
                ins.then_inc(t_bc.sem, 1)

            Yb = Y[:, :].bitcast(BF16)

            def spread(e, b):
                if e == 0:
                    pe.wait_ge(bcT_ready.sem, bcT_ready.at(b, 1))
                    pe.wait_ge(delta_ready.sem, delta_ready.at(b, 1))
                for part in range(2):
                    if part == 0 and e >= 2:
                        pe.wait_ge(hc_ready.sem, hc_ready.at(b, CH * (e - 1)))
                    if part == 1 and e >= 1:
                        pe.wait_ge(dbu_ready.sem, dbu_ready.at(b, CH * e))
                    for k in range(2):
                        s = part * STATE + 2 * e + k
                        ins = mm(R[(2 * e + part) % 3][:, k * BT:(k + 1) * BT],
                                 pick[:, s:s + 1].broadcast_to([HALF, P]), bcT[:, :])
                    ins.then_inc(bcast_mm.sem, 1)

            def scan_out(b):
                pe.wait_ge(yz_ready.sem, yz_ready.at(b, CH))
                for u in range(U):
                    for c in range(CH):
                        ins = mm(R[1][:, u * DIM:(u + 1) * DIM], yy[:, c, u * P:(u + 1) * P], out_w[:, c, :],
                                 c == 0, c == CH - 1)
                ins.then_inc(out_mm.sem, 1)

            def turn_h4(b):
                pe.wait_ge(h4_ready.sem, h4_ready.at(b, 1))
                turn(h4, R[2], t_h4)

            def gate1(b):
                pe.wait_ge(h4T_ready.sem, h4T_ready.at(b, 1))
                for u in range(U):
                    for kk in range(2):
                        ins = mm(R[0][:, u * 8:u * 8 + 8], h4T[:, kk, u * P:(u + 1) * P], gate1_w[:, kk, :],
                                 kk == 0, kk == 1)
                ins.then_inc(gate1_mm.sem, 1)

            def ffn_in(e, b):
                if e == 1:
                    pe.wait_ge(th_ready.sem, th_ready.at(b, 1))
                if e >= 2:
                    pe.wait_ge(gg_ready.sem, gg_ready.at(b, e - 1))
                for at, w in ((0, f1_w), (BT, f3_w)):
                    for kk in range(2):
                        ins = mm(R[(e + 1) % 2][:, at:at + BT], w[:, kk, e * INTER:(e + 1) * INTER],
                                 h4T[:, kk, :], kk == 0, kk == 1)
                ins.then_inc(f13_mm.sem, 1)

            def ffn_out(e, b):
                pe.wait_ge(gg_ready.sem, gg_ready.at(b, e + 1))
                if e:
                    pe.wait_ge(fy_taken.sem, fy_taken.at(b, e))
                for u in range(U):
                    ins = mm(R[2][:, u * DIM:(u + 1) * DIM], gg[e % 2][:, u * P:(u + 1) * P], f2_w[:, e, :])
                ins.then_inc(fy_mm.sem, 1)

            def step(a, m, b):
                if m is not None:
                    turn_z2(m)
                if a is not None:
                    tok(a)
                if m is not None:
                    hidden(0, m)
                    gate(m)
                if b is not None:
                    spread(0, b)
                if a is not None:
                    tok_squares(a)
                if m is not None:
                    hidden(1, m)
                if a is not None:
                    turn_input(0, a)
                if b is not None:
                    spread(1, b)
                if m is not None:
                    gate_bias(m)
                    expert_out(0, m)
                if a is not None:
                    queries_keys(0, a)
                if m is not None:
                    hidden(2, m)
                if a is not None:
                    values(0, a)
                if b is not None:
                    spread(2, b)
                if m is not None:
                    expert_out(1, m)
                if a is not None:
                    scores(0, a)
                if m is not None:
                    hidden(3, m)
                if a is not None:
                    weigh_values(0, a)
                if b is not None:
                    spread(3, b)
                if m is not None:
                    expert_out(2, m)
                if a is not None:
                    project(0, a)
                if m is not None:
                    hidden(4, m)
                if a is not None:
                    turn_input(1, a)
                if b is not None:
                    spread(4, b)
                if m is not None:
                    expert_out(3, m)
                if a is not None:
                    queries_keys(1, a)
                if m is not None:
                    hidden(5, m)
                if a is not None:
                    values(1, a)
                if b is not None:
                    spread(5, b)
                if a is not None:
                    scores(1, a)
                if m is not None:
                    expert_out(4, m)
                    hidden(6, m)
                if b is not None:
                    spread(6, b)
                if m is not None:
                    expert_out(5, m)
                if b is not None:
                    spread(7, b)
                if a is not None:
                    weigh_values(1, a)
                if m is not None:
                    hidden(7, m)
                    expert_out(6, m)
                if a is not None:
                    project(1, a)
                if b is not None:
                    scan_out(b)
                if m is not None:
                    expert_out(7, m)
                if b is not None:
                    turn_h4(b)
                    gate1(b)
                if m is not None:
                    turn_h3(m)
                    xz(m)
                if b is not None:
                    ffn_in(0, b)
                    ffn_in(1, b)
                    ffn_out(0, b)
                    ffn_in(2, b)
                    ffn_out(1, b)
                    ffn_in(3, b)
                    ffn_out(2, b)
                if m is not None:
                    bc_dt(m)
                if b is not None:
                    ffn_in(4, b)
                    ffn_out(3, b)
                    ffn_in(5, b)
                    ffn_out(4, b)
                if m is not None:
                    dt(m)
                if b is not None:
                    ffn_in(6, b)
                    ffn_out(5, b)
                if m is not None:
                    turn_bc(m)
                if b is not None:
                    ffn_in(7, b)
                    ffn_out(6, b)
                    ffn_in(8, b)
                    ffn_out(7, b)
                    ffn_out(8, b)

            step(0, None, None)
            step(1, 0, None)
            with pe.Fori(1, BLOCKS - 1) as i:
                step(i + 1, i, i - 1)
            step(None, BLOCKS - 1, BLOCKS - 2)
            step(None, None, BLOCKS - 1)

        @block.scalar
        def _(act):
            act.wait_ge(ld["cst"].sem, 32)
            act.wait_ge(ld["rows"].sem, 64)

            def two(ap):
                return ap.rearrange("p (u e) -> p u e", u=U)

            def two96(bank_):
                return bank_[0:HALF, :].rearrange("p (h t) -> p h t", h=2)

            def gain_bias(dst, src, gb):
                for h in range(2):
                    ins = act.activation(dst[:, h, :], src[:, h, :], ACT.Identity,
                                         scale=gb[:, h:h + 1], bias=gb[:, 2 + h:3 + h])
                return ins

            def squares(a):
                act.wait_ge(x_loaded.sem, x_loaded.at(a, 16))
                act.activation(sq[:, :, :], xb[:, :, :], ACT.Square).then_inc(sq_ready.sem, 1)

            def turned_h0(a):
                act.wait_ge(t_a.sem, t_a.at(a, 1))
                act.activation(hT[:, :, :], two96(X1), ACT.Copy).then_inc(tc_a.sem, 1)

            def turned_z1(a):
                act.wait_ge(t_a.sem, t_a.at(a, 2))
                gain_bias(hT, two96(X1), ln1_gb).then_inc(tc_a.sem, 1)

            def turned_heads(n, a):
                act.wait_ge(pv_mm.sem, pv_mm.at(a, n + 1))
                act.activation(oT[:, :, :], two96(X1), ACT.Copy).then_inc(tc_a.sem, 1)

            def queries_keys(a):
                act.wait_ge(qk_mm.sem, qk_mm.at(a, 2))
                act.activation(qT[:, :, :], two96(X0), ACT.Copy).then_inc(q_ready.sem, 1)
                act.activation(kT[:, :, :], two96(X1), ACT.Copy).then_inc(k_ready.sem, 1)

            def values(n, a):
                act.wait_ge(v_mm.sem, v_mm.at(a, n + 1))
                for k in range(2):
                    cols_ = slice(k * HD, (k + 1) * HD)
                    ins = act.activation(
                        vx[:, :, :, :].rearrange("p u (j k) e -> p (u j) k e", k=2)[:, :, k, cols_],
                        X0[:, 0:U * DIM].rearrange("p (j e) -> p j e", e=2 * HD)[:, :, cols_], ACT.Copy)
                ins.then_inc(v_ready.sem, 1)

            def softmax_exp(a):
                act.wait_ge(sm_in.sem, sm_in.at(a, 1))
                act.activation(pm[:, :, :, :], pm[:, :, :, :], ACT.Exp, scale=HD ** -0.5
                               ).then_inc(sm_out.sem, 1)

            def turned_z2(m):
                act.wait_ge(t_z2.sem, t_z2.at(m, 1))
                if first(m):
                    act.wait_ge(ld["gate0"].sem, 48)
                gain_bias(h2T, Y[:, :].rearrange("p (h t) -> p h t", h=2), ln2_gb).then_inc(h2T_ready.sem, 1)

            def gate_exp(m):
                act.wait_ge(gate_in.sem, gate_in.at(m, 1))
                act.activation(ge[:, :, :], gd[:, :, :], ACT.Exp).then_inc(gate_out.sem, 1)

            def round_w1(e, mp, m):
                if mp == 0:
                    act.wait_ge(w1_loaded.sem, w1_loaded.at(m, 16 * (e + 1)))
                act.activation(w1_hi[(e * HM // 2 + mp) % RING][:, :, :],
                               w1_raw[:, :, 2 * mp * P:2 * (mp + 1) * P], ACT.Copy).then_inc(w1_rounded.sem, 1)

            def round_first_w1(m):
                for mp in range(HM // 2):
                    round_w1(0, mp, m)

            def gelu(e, m):
                if e >= 2:
                    act.wait_ge(y_mm.sem, y_mm.at(m, e - 1))
                for mp in range(HM // 2):
                    unit = e * HM // 2 + mp
                    act.wait_ge(hid_mm.sem, hid_mm.at(m, unit + 1))
                    for k in range(2):
                        at = 2 * mp + k
                        ins = act.activation(he[e % 2][:, at, :], (H0, H1)[unit % 2][:, k * BT:(k + 1) * BT],
                                             ACT.Gelu, bias=b1[:, e * HM + at:e * HM + at + 1])
                    ins.then_inc(hid_ready.sem, 1)
                    if e + 1 < EXPERTS:
                        round_w1(e + 1, mp, m)

            def turned_h3(m):
                act.wait_ge(t_h3.sem, t_h3.at(m, 1))
                act.activation(h3T[:, :, :], two96(H1), ACT.Copy).then_inc(h3T_ready.sem, 1)

            def xz(m):
                act.wait_ge(xz_mm.sem, xz_mm.at(m, 1))
                for c in range(CH):
                    src = (H0, H1)[c // 2][:, (c % 2) * BT:(c % 2 + 1) * BT].rearrange("p (b n) -> p b n", b=BI)
                    if c == 2:
                        act.wait_ge(xz_mm.sem, xz_mm.at(m, 2))
                    ins = act.activation(xpad[:, c, :, TAPS - 1:], src, ACT.Copy)
                ins.then_inc(xpad_ready.sem, 1)
                for c in range(CH):
                    k = CH + c
                    ins = act.activation(sz[:, c, :], (H0, H1, Y)[k // 2][:, (k % 2) * BT:(k % 2 + 1) * BT],
                                         ACT.Silu)
                ins.then_inc(z_ready.sem, 1)

            def u_silu(m):
                act.wait_ge(uc_ready.sem, uc_ready.at(m, 1))
                for c in range(CH):
                    ins = act.activation(uu[:, c, :], uc[:, c, :], ACT.Silu,
                                         bias=cols[:, c, TAPS:TAPS + 1])
                ins.then_inc(u_ready.sem, 1)

            def dt_first(m):
                act.wait_ge(dtp_mm.sem, dtp_mm.at(m, 1))
                act.activation(dtp[:, 0:2, :], H0[:, :].rearrange("p (m t) -> p m t", m=2), ACT.Copy)
                act.activation(dtp[:, 2, :], H1[:, 0:BT], ACT.Copy).then_inc(dtp_ready.sem, 1)

            def bc_exp(m):
                act.wait_ge(bc_in.sem, bc_in.at(m, 1))
                act.activation(be[:, :, :], bd[:, :, :], ACT.Exp).then_inc(bc_out.sem, 1)

            def softplus_in(m):
                act.wait_ge(dt_mm.sem, dt_mm.at(m, 1))
                for c in range(CH):
                    src = (X0, X1)[c // 2][:, (c % 2) * BT:(c % 2 + 1) * BT]
                    act.activation(delta[:, c, :], src, ACT.Relu, bias=cols[:, c, TAPS + 1:TAPS + 2])
                    ins = act.activation(dab[:, c, :], src, ACT.Abs, bias=cols[:, c, TAPS + 1:TAPS + 2])
                ins.then_inc(abs_done.sem, 1)

            def softplus_out(m):
                act.wait_ge(abs_done.sem, abs_done.at(m, 1))
                act.activation(dab[:, :, :], dab[:, :, :], ACT.Exp, scale=-1.0).then_inc(exp_done.sem, 1)
                act.wait_ge(exp_done.sem, exp_done.at(m, 1))
                act.activation(dab[:, :, :], dab[:, :, :], ACT.Ln, bias=1.0).then_inc(sp_ready.sem, 1)

            def turned_bc(m):
                act.wait_ge(t_bc.sem, t_bc.at(m, 1))
                act.activation(bcT[:, :], Yb[0:HALF, 0:BT], ACT.Copy).then_inc(bcT_ready.sem, 1)

            Yb = Y[:, :].bitcast(BF16)

            def decays(e, b):
                if e == 0:
                    act.wait_ge(delta_ready.sem, delta_ready.at(b, 1))
                for c in range(CH):
                    n = e * CH + c
                    if n >= 3:
                        act.wait_ge(scan_ready.sem, scan_ready.at(b, n - 2))
                    for k in range(2):
                        ins = act.activation(
                            dA[n % 3][:, k * BI:(k + 1) * BI, 1:],
                            delta[:, c, :].rearrange("p (b n) -> p b n", b=BI)[:, :, 1:], ACT.Exp,
                            scale=decay[:, c, 2 * e + k:2 * e + k + 1])
                    ins.then_inc(dA_ready.sem, 1)

            def turned_h4(b):
                act.wait_ge(t_h4.sem, t_h4.at(b, 1))
                act.activation(h4T[:, :, :], two96(R[2]), ACT.Copy).then_inc(h4T_ready.sem, 1)

            def gate1_tanh(b):
                act.wait_ge(gate1_mm.sem, gate1_mm.at(b, 1))
                act.activation(th[:, :, :], two(R[0][:, 0:16]), ACT.Tanh, scale=0.5).then_inc(th_ready.sem, 1)

            def ffn_silu(e, b):
                act.wait_ge(f13_mm.sem, f13_mm.at(b, e + 1))
                if e >= 2:
                    act.wait_ge(gg_ready.sem, gg_ready.at(b, e - 1))
                act.activation(sg[e % 2][:, :], R[(e + 1) % 2][:, 0:BT], ACT.Silu).then_inc(sg_ready.sem, 1)

            act.activation(decay[:, :, :], cols[:, :, TAPS + 2:], ACT.Exp).then_inc(exp_a.sem, 1)

            def step(a, m, b):
                if m is not None:
                    turned_z2(m)
                if a is not None:
                    squares(a)
                if m is not None:
                    gelu(0, m)
                    gate_exp(m)
                if b is not None:
                    decays(0, b)
                if m is not None:
                    gelu(1, m)
                if a is not None:
                    turned_h0(a)
                if b is not None:
                    decays(1, b)
                if m is not None:
                    gelu(2, m)
                if a is not None:
                    values(0, a)
                if b is not None:
                    decays(2, b)
                if m is not None:
                    gelu(3, m)
                if a is not None:
                    turned_heads(0, a)
                if b is not None:
                    decays(3, b)
                if m is not None:
                    gelu(4, m)
                if a is not None:
                    turned_z1(a)
                if b is not None:
                    decays(4, b)
                if a is not None:
                    queries_keys(a)
                if m is not None:
                    gelu(5, m)
                if a is not None:
                    values(1, a)
                if b is not None:
                    decays(5, b)
                if a is not None:
                    softmax_exp(a)
                if m is not None:
                    gelu(6, m)
                if b is not None:
                    decays(6, b)
                    decays(7, b)
                if a is not None:
                    turned_heads(1, a)
                if m is not None:
                    gelu(7, m)
                if b is not None:
                    turned_h4(b)
                    gate1_tanh(b)
                if m is not None:
                    turned_h3(m)
                    xz(m)
                if b is not None:
                    ffn_silu(0, b)
                    ffn_silu(1, b)
                if m is not None:
                    u_silu(m)
                if b is not None:
                    ffn_silu(2, b)
                    ffn_silu(3, b)
                if m is not None:
                    dt_first(m)
                if b is not None:
                    ffn_silu(4, b)
                    ffn_silu(5, b)
                if m is not None:
                    bc_exp(m)
                    softplus_in(m)
                if b is not None:
                    ffn_silu(6, b)
                if m is not None:
                    turned_bc(m)
                if b is not None:
                    ffn_silu(7, b)
                    ffn_silu(8, b)
                if a is not None:
                    round_first_w1(a)
                if m is not None:
                    softplus_out(m)

            step(0, None, None)
            act.wait_ge(neg_a.sem, 1)
            step(1, 0, None)
            with act.Fori(1, BLOCKS - 1) as i:
                step(i + 1, i, i - 1)
            step(None, BLOCKS - 1, BLOCKS - 2)
            step(None, None, BLOCKS - 1)

        @block.vector
        def _(dve):
            V = nc.vector
            ca, cm, cs, cb = (Chain(dve, s) for s in (dve_a, dve_m, dve_s, dve_b))

            V.memset(ones[:, :], 1.0)
            V.memset(half_neg[:, :], -0.5)
            for n in range(3):
                V.memset(dA[n][:, :, 0:1], 0.0)
            V.memset(xpad[:, :, :, 0:TAPS - 1], 0.0)
            dve.wait_ge(ld["cst"].sem, 32)
            V.tensor_copy(tokw[:, :, DIM:DIM + 1], cnt.unsqueeze(2))
            V.tensor_copy(identb[:, :], ident)
            for part in range(3):
                ins = V.tensor_copy(pick[32 * part:32 * part + 32, :], ident[0:32, 0:32])
            ins.then_inc(ready.sem, 1)
            for s in range(SHIFTS):
                dve.wait_ge(ld[f"tok{s}"].sem, 16)
                for k in range(PK):
                    gain, w, o = tokgb[:, 0, s, k:k + 1], wraw[:, s, k, :], tokw[:, k, 0:DIM]
                    if s == 0:
                        ins = V.tensor_scalar(o, w, gain, None, ALU.mult)
                    else:
                        ins = V.scalar_tensor_tensor(out=o, in0=w, scalar=gain, in1=o, op0=ALU.mult, op1=ALU.add)
                if s < SHIFTS - 1:
                    ins.then_inc(tokw_part.sem, 1)
                    dve.wait_ge(tokw_part.sem, s + 1)
            ins.then_inc(tokw_ready.sem, 1)
            V.memset(vx[:, :, :, :], 0.0)
            V.memset(pbd[:, :, :], 0.0)
            dve.wait_ge(ld["rows"].sem, 64)
            dve.wait_ge(beta_mm.sem, 1)
            V.tensor_tensor(tok_bw[:, :], H0[:, 0:DIM], tok_b, ALU.add)
            dve.wait_ge(colsum_mm.sem, 1)
            V.tensor_copy(tok_cs[:, :], H1[:, 0:DIM]).then_inc(ready.sem, 1)
            dve.wait_ge(ready.sem, 2)
            dve.wait_ge(exp_a.sem, 1)
            V.tensor_scalar(decay[:, :, :], decay[:, :, :], -1.0, None, ALU.mult).then_inc(neg_a.sem, 1)

            def norm(i, ch, src, dst, k, var, rs, bufs, done):
                st_, mv_, ve_, rstd_ = bufs
                for u in range(U):
                    n = ch.step(V.bn_stats(st_[:, u, :], src[:, u, :]))
                ch.after(n)
                V.memset(idle[:, :], 0.0)
                for u in range(U):
                    n = ch.step(V.bn_aggr(mv_[:, u, :], st_[:, u, :]))
                ch.after(n)
                V.tensor_scalar(ve_[:, :], mv_[:, :, 1], EPS, None, ALU.add).then_inc(var.sem, 1)
                dve.wait_ge(rs.sem, rs.at(i, k))
                for u in range(U):
                    ins = V.tensor_scalar(dst[:, u, 0:DIM], src[:, u, :], mv_[:, u, 0:1], rstd_[:, u:u + 1],
                                          ALU.subtract, ALU.mult)
                    if dst is z and src is xm:
                        ins = V.tensor_scalar(dst[:, u, DIM:], src[:, u, P:], mv_[:, u, 0:1], rstd_[:, u:u + 1],
                                              ALU.subtract, ALU.mult)
                if done is None:
                    ch.link(ins)
                else:
                    ins.then_inc(done.sem, 1)

            ab, mb, bb = (st, mv, ve, rstd), (stm, mvm, vem, rstdm), (stb, mvb, veb, rstdb)

            def two(ap):
                return ap.rearrange("p (u e) -> p u e", u=U)

            def tok(a):
                ca.start(a)
                dve.wait_ge(tok_mm.sem, tok_mm.at(a, 2))
                sums = X0[:, DIM:2 * (DIM + 1):DIM + 1]
                ca.link(V.tensor_scalar(mv[:, :, 0], sums, -1.0 / PATCH_DIM, None, ALU.mult))
                ca.link(V.tensor_tensor(mv[:, :, 1], mv[:, :, 0], mv[:, :, 0], ALU.mult))
                squares_sum = X0[:, U * (DIM + 1):U * (DIM + 1) + U]
                ca.link(V.scalar_tensor_tensor(out=ve[:, :], in0=squares_sum, scalar=1.0 / PATCH_DIM,
                                               in1=mv[:, :, 1], op0=ALU.mult, op1=ALU.subtract))
                V.tensor_scalar(ve[:, :], ve[:, :], EPS, None, ALU.add).then_inc(var_a.sem, 1)
                for u in range(U):
                    n = ca.step(V.scalar_tensor_tensor(
                        out=tmp[:, u, :], in0=tok_cs[:, :], scalar=mv[:, u, 0:1],
                        in1=X0[:, u * (DIM + 1):u * (DIM + 1) + DIM], op0=ALU.mult, op1=ALU.add))
                ca.after(n)
                dve.wait_ge(rstd_a.sem, rstd_a.at(a, 1))
                for u in range(U):
                    ins = V.scalar_tensor_tensor(out=h0[:, u, :], in0=tmp[:, u, :], scalar=rstd[:, u:u + 1],
                                                 in1=tok_bw[:, :], op0=ALU.mult, op1=ALU.add)
                ins.then_inc(h_a.sem, 1)

            def qk_l1(a):
                dve.wait_ge(qk_mm.sem, qk_mm.at(a, 1))
                for n, b in ((0, X0), (1, X1)):
                    last = ca.step(V.tensor_reduce(
                        l1[:, :, n * BI:(n + 1) * BI], b[0:HALF, :].rearrange("p (m b n) -> p m b n", m=2, b=BI),
                        AX.X, ALU.add, apply_absolute_value=True))
                ca.after(last)
                ca.link(V.tensor_scalar(l1[:, :, :], l1[:, :, :], 1e-12, None, ALU.max))
                ca.link(V.reciprocal(l1[:, :, :], l1[:, :, :]))
                for n, b, o, sig in ((1, X1, kT, k_ready), (0, X0, qT, q_ready)):
                    for m in range(2):
                        ins = V.tensor_tensor(
                            o[:, m, :].rearrange("p (b n) -> p b n", b=BI),
                            b[0:HALF, m * BT:(m + 1) * BT].rearrange("p (b n) -> p b n", b=BI),
                            l1[:, m, n * BI:(n + 1) * BI].unsqueeze(2).broadcast_to([HALF, BI, SEQ]), ALU.mult)
                    ins.then_inc(sig.sem, 1)

            def spread_keys(n, a):
                dve.wait_ge(k_ready.sem, k_ready.at(a, n + 1))
                for h in range(HH):
                    ins = V.tensor_scalar(kx[:, :, h, :], kT[:, :, :], cst[0:HALF, C_HEAD + h:C_HEAD + h + 1],
                                          None, ALU.mult)
                ins.then_inc(kx_ready.sem, 1)

            def to_block_diagonal():
                for g in range(4):
                    r = slice(32 * g, 32 * g + 32)
                    ins = V.transpose(pbd[r, :, r], pm[r, :, :, :].rearrange("p u h j -> p (u h) j"))
                ins.then_inc(pbd_ready.sem, 1)

            def linear_mask(a):
                dve.wait_ge(s_mm.sem, s_mm.at(a, 1))
                for u, b in ((0, X0), (1, X1)):
                    n = ca.step(V.tensor_tensor(
                        pm[:, u, :, :], b[:, 0:HEADS * 32].rearrange("p (h j) -> p h j", h=HEADS),
                        mask.unsqueeze(1).broadcast_to([P, HEADS, 32]), ALU.mult))
                ca.after(n)
                to_block_diagonal()

            def after_linear(a):
                dve.wait_ge(proj_mm.sem, proj_mm.at(a, 1))
                dve.wait_ge(h0b_ready.sem, h0b_ready.at(a, 1))
                ca.link(V.tensor_tensor(tmp[:, :, :], two(X0[:, 0:U * DIM]), hb[:, :, :], ALU.add))
                norm(a, ca, tmp, h1, 2, var_a, rstd_a, ab, h1_ready)
                dve.wait_ge(h1_ready.sem, h1_ready.at(a, 1))
                norm(a, ca, h1, z, 3, var_a, rstd_a, ab, h_a)

            def softmax_in(a):
                dve.wait_ge(s_mm.sem, s_mm.at(a, 2))
                for u, b in ((0, X0), (1, X1)):
                    n = ca.step(V.tensor_tensor(
                        pm[:, u, :, :], b[:, 0:HEADS * 32].rearrange("p (h j) -> p h j", h=HEADS),
                        neg.unsqueeze(1).broadcast_to([P, HEADS, 32]), ALU.add))
                ca.after(n)
                flat = pm[:, :, :, :].rearrange("p u h j -> p (u h) j")
                ca.link(V.tensor_reduce(mx[:, :], flat, AX.X, ALU.max))
                V.tensor_tensor(flat, flat, mx[:, :].unsqueeze(2).broadcast_to([P, U * HEADS, 32]),
                                ALU.subtract).then_inc(sm_in.sem, 1)

            def softmax_out(a):
                flat = pm[:, :, :, :].rearrange("p u h j -> p (u h) j")
                dve.wait_ge(sm_out.sem, sm_out.at(a, 1))
                ca.link(V.tensor_reduce(mx[:, :], flat, AX.X, ALU.add))
                ca.link(V.reciprocal(mx[:, :], mx[:, :]))
                ca.link(V.tensor_tensor(flat, flat, mx[:, :].unsqueeze(2).broadcast_to([P, U * HEADS, 32]),
                                        ALU.mult))
                to_block_diagonal()

            def after_softmax(a):
                dve.wait_ge(proj_mm.sem, proj_mm.at(a, 2))
                dve.wait_ge(h1b_ready.sem, h1b_ready.at(a, 1))
                V.tensor_tensor(xm[:, :, :], two(X0[:, 0:U * DIM]), hb[:, :, :], ALU.add).then_inc(xm_ready.sem, 1)
                dve.wait_ge(xm_ready.sem, xm_ready.at(a, 1))
                norm(a, ca, xm, z, 4, var_a, rstd_a, ab, h_a)
                ca.end()

            def ranks(ch, vals, n, rk_, req_, rank_):
                a = vals.unsqueeze(2).broadcast_to([P, U, n, n])
                b = vals.unsqueeze(3).broadcast_to([P, U, n, n])
                ch.step(V.tensor_tensor(rk_[:, :, 0:n, 0:n], a, b, ALU.is_gt))
                ch.link(V.tensor_tensor(req_[:, :, 0:n, 0:n], a, b, ALU.is_equal))
                ch.link(V.tensor_tensor(req_[:, :, 0:n, 0:n], req_[:, :, 0:n, 0:n],
                                        tri[:, 0:n, 0:n].unsqueeze(1).broadcast_to([P, U, n, n]), ALU.mult))
                ch.link(V.tensor_tensor(rk_[:, :, 0:n, 0:n], rk_[:, :, 0:n, 0:n], req_[:, :, 0:n, 0:n], ALU.add))
                ch.link(V.tensor_reduce(rank_[:, :, 0:n], rk_[:, :, 0:n, 0:n], AX.X, ALU.add))
                ch.link(V.tensor_scalar(rank_[:, :, 0:n], rank_[:, :, 0:n], 1.5, None, ALU.is_lt))

            def over8(ap):
                return ap.broadcast_to([P, U, 8])

            def split_h2(m):
                dve.wait_ge(h2T_ready.sem, h2T_ready.at(m, 1))
                V.tensor_copy(h2_hi[:, :], h2T[:, 0, :])
                V.tensor_copy(h2_rest[:, :], h2T[:, 1, :]).then_inc(h2_rounded.sem, 1)
                dve.wait_ge(h2_rounded.sem, h2_rounded.at(m, 1))
                V.tensor_tensor(h2_lo[:, :], h2T[:, 0, :], h2_hi[:, :].bitcast(F32), ALU.subtract)
                V.tensor_tensor(h2_rest[REST:P, :], h2T[REST:P, 1, :], h2_rest[REST:P, :].bitcast(F32),
                                ALU.subtract).then_inc(h2_ready.sem, 1)

            def gate(m):
                cm.start(m)
                dve.wait_ge(gate_mm.sem, gate_mm.at(m, 1))
                cm.link(V.tensor_tensor(lg[:, :, :], two(Y[:, 0:16]), gate0_b.unsqueeze(1).broadcast_to([P, U, 8]),
                                        ALU.add))
                cm.link(V.tensor_reduce(g1[:, :, :], lg[:, :, :], AX.X, ALU.max))
                V.tensor_tensor(gd[:, :, :], lg[:, :, :], over8(g1[:, :, :]), ALU.subtract).then_inc(gate_in.sem, 1)
                ranks(cm, lg[:, :, :], 8, rk, req, rank)
                dve.wait_ge(gate_out.sem, gate_out.at(m, 1))
                cm.link(V.tensor_tensor(cw[:, :, :], ge[:, :, :], rank[:, :, :], ALU.mult))
                cm.link(V.tensor_reduce(g1[:, :, :], cw[:, :, :], AX.X, ALU.add))
                cm.link(V.reciprocal(g1[:, :, :], g1[:, :, :]))
                V.tensor_tensor(cw[:, :, :], cw[:, :, :], over8(g1[:, :, :]), ALU.mult).then_inc(cw_ready.sem, 1)

            def gate_bias(m):
                dve.wait_ge(cwT_mm.sem, cwT_mm.at(m, 1))
                V.tensor_copy(cwT[:, :], Y[0:8, 0:BT]).then_inc(cwT_ready.sem, 1)
                dve.wait_ge(b2_mm.sem, b2_mm.at(m, 1))
                dve.wait_ge(hx_ready.sem, hx_ready.at(m, 1))
                V.tensor_tensor(acc[:, :, :], two(Y[:, 0:U * DIM]), acc[:, :, :], ALU.add
                                ).then_inc(acc0_ready.sem, 1)

            def add_expert(e, m):
                dve.wait_ge(y_mm.sem, y_mm.at(m, e + 1))
                if e == 0:
                    dve.wait_ge(acc0_ready.sem, acc0_ready.at(m, 1))
                else:
                    dve.wait_ge(y_taken.sem, y_taken.at(m, e))
                y = H0 if e == EXPERTS - 1 else Y
                for u in range(U):
                    ins = V.scalar_tensor_tensor(out=acc[:, u, :], in0=y[:, u * DIM:(u + 1) * DIM],
                                                 scalar=cw[:, u, e:e + 1], in1=acc[:, u, :],
                                                 op0=ALU.mult, op1=ALU.add)
                ins.then_inc(y_taken.sem, 1)

            def after_experts(m):
                dve.wait_ge(y_taken.sem, y_taken.at(m, EXPERTS))
                norm(m, cm, acc, h3, 1, var_m, rstd_m, mb, h3_ready)
                cm.end()

            uc4 = uc.rearrange("p c (b n) -> p c b n", b=BI)

            def conv(m):
                cs.start(m)
                dve.wait_ge(xpad_ready.sem, xpad_ready.at(m, 1))
                last = [0] * CH
                for k in range(TAPS):
                    for c in range(CH):
                        if k:
                            cs.after(last[c])
                        src, w = xpad[:, c, :, k:k + SEQ], cols[:, c, k:k + 1]
                        if k == 0:
                            ins = V.tensor_scalar(uc4[:, c, :, :], src, w, None, ALU.mult)
                        else:
                            ins = V.scalar_tensor_tensor(out=uc4[:, c, :, :], in0=src, scalar=w, in1=uc4[:, c, :, :],
                                                         op0=ALU.mult, op1=ALU.add)
                        if (k, c) == (TAPS - 1, CH - 1):
                            ins.then_inc(uc_ready.sem, 1)
                        else:
                            last[c] = cs.step(ins)

            def bc_split(m):
                dve.wait_ge(bc_mm.sem, bc_mm.at(m, 1))
                src = two(Y[:, 0:64])
                cs.step(V.tensor_copy(bcf[:, :, STATE:], src[:, :, STATE:]))
                cs.link(V.tensor_reduce(bm[:, :, :], src[:, :, 0:STATE], AX.X, ALU.max))
                V.tensor_tensor(bd[:, :, :], src[:, :, 0:STATE], bm[:, :, :].broadcast_to([P, U, STATE]),
                                ALU.subtract).then_inc(bc_in.sem, 1)

            def bc_parts(m):
                dve.wait_ge(bc_out.sem, bc_out.at(m, 1))
                cs.link(V.tensor_reduce(bm[:, :, :], be[:, :, :], AX.X, ALU.add))
                cs.link(V.reciprocal(bm[:, :, :], bm[:, :, :]))
                cs.link(V.tensor_tensor(bcf[:, :, 0:STATE], be[:, :, :], bm[:, :, :].broadcast_to([P, U, STATE]),
                                        ALU.mult))
                cs.link(V.tensor_copy(bc3[:, :, 0, :], bcf[:, :, :]))
                cs.link(V.tensor_tensor(bres[:, :, :], bcf[:, :, :], bc3[:, :, 0, :], ALU.subtract))
                cs.link(V.tensor_copy(bc3[:, :, 1, :], bres[:, :, :]))
                V.tensor_tensor(bc3[:, :, 2, :], bres[:, :, :], bc3[:, :, 1, :], ALU.subtract
                                ).then_inc(bc3_ready.sem, 1)

            def softplus(m):
                dve.wait_ge(sp_ready.sem, sp_ready.at(m, 1))
                V.tensor_tensor(delta[:, :, :], delta[:, :, :], dab[:, :, :], ALU.add).then_inc(delta_ready.sem, 1)
                cs.end()

            def wide(ap):
                return ap.unsqueeze(1).broadcast_to([P, 2, BT])

            def flat2(ap):
                return ap.rearrange("p (k t) -> p k t", k=2)

            def scan_step(n, stage, b):
                sp2, c = divmod(n, CH)

                if stage == 0:
                    if n == 0:
                        dve.wait_ge(du_ready.sem, du_ready.at(b, 1))
                    if c == 0:
                        dve.wait_ge(bcast_mm.sem, bcast_mm.at(b, 2 * sp2 + 1))
                    if n >= SLOTS:
                        dve.wait_ge(y_added.sem, y_added.at(b, n - SLOTS + 1))
                    V.tensor_tensor(flat2(hs[n % SLOTS][:, :]), flat2(R[2 * sp2 % 3][:, :]), wide(du[:, c, :]),
                                    ALU.mult).then_inc(dbu_ready.sem, 1)
                elif stage == 1:
                    dve.wait_ge(dbu_ready.sem, dbu_ready.at(b, n + 1))
                    dve.wait_ge(dA_ready.sem, dA_ready.at(b, n + 1))
                    V.tensor_tensor_scan(hs[n % SLOTS][:, :], dA[n % 3][:, :, :].rearrange("p x n -> p (x n)"),
                                         hs[n % SLOTS][:, :], 0.0, ALU.mult, ALU.add
                                         ).then_inc(scan_ready.sem, 1)
                else:
                    if c == 0:
                        dve.wait_ge(bcast_mm.sem, bcast_mm.at(b, 2 * sp2 + 2))
                    dve.wait_ge(scan_ready.sem, scan_ready.at(b, n + 1))
                    V.tensor_tensor(hs[n % SLOTS][:, :], hs[n % SLOTS][:, :], R[(2 * sp2 + 1) % 3][:, :], ALU.mult
                                    ).then_inc(hc_ready.sem, 1)

            def scan_part(e, b):
                for n in range(CH * e, CH * e + CH):
                    scan_step(n, 0, b)
                    if n >= 1:
                        scan_step(n - 1, 1, b)
                    if n >= 2:
                        scan_step(n - 2, 2, b)
                if e == STATE // 2 - 1:
                    scan_step(STEPS - 1, 1, b)
                    scan_step(STEPS - 2, 2, b)
                    scan_step(STEPS - 1, 2, b)

            def after_scan(b):
                cb.start(b)
                dve.wait_ge(kept.sem, kept.at(b, 1))
                dve.wait_ge(out_mm.sem, out_mm.at(b, 1))
                V.tensor_tensor(rb[:, :, :], two(R[1][:, 0:U * DIM]), rb[:, :, :], ALU.add).then_inc(scanned.sem, 1)
                dve.wait_ge(scanned.sem, scanned.at(b, 1))
                norm(b, cb, rb, h4, 1, var_b, rstd_b, bb, h4_ready)

            def gate1(b):
                dve.wait_ge(th_ready.sem, th_ready.at(b, 1))
                cb.link(V.tensor_scalar(sc[:, :, :], th[:, :, :], 0.5, 0.5, ALU.mult, ALU.add))
                cb.link(V.tensor_tensor(sbias[:, :, :], sc[:, :, :], gate1_b.unsqueeze(1).broadcast_to([P, U, 8]),
                                        ALU.add))
                pairs = sbias[:, :, :].rearrange("p u (g k) -> p u g k", k=2)
                cb.link(V.tensor_tensor(gs[:, :, :], pairs[:, :, :, 0], pairs[:, :, :, 1], ALU.add))
                ranks(cb, gs[:, :, :], 4, b_rk, b_req, b_rank)
                cb.link(V.tensor_scalar(gr[:, :, :], b_rank[:, :, 0:4], 1.0, FAR, ALU.subtract, ALU.mult))
                cb.link(V.tensor_tensor(pairs, pairs, gr[:, :, :].unsqueeze(3).broadcast_to([P, U, 4, 2]), ALU.add))
                ranks(cb, sbias[:, :, :], 8, b_rk, b_req, b_rank)
                cb.link(V.tensor_tensor(cw2[:, :, :], sc[:, :, :], b_rank[:, :, :], ALU.mult))
                cb.link(V.tensor_reduce(b_g1[:, :, :], cw2[:, :, :], AX.X, ALU.add))
                cb.link(V.tensor_scalar(b_g1[:, :, :], b_g1[:, :, :], 1e-6, None, ALU.add))
                cb.link(V.reciprocal(b_g1[:, :, :], b_g1[:, :, :]))
                cb.link(V.tensor_tensor(cw2[:, :, :], cw2[:, :, :], over8(b_g1[:, :, :]), ALU.mult))

            def ffn_mul(e, b):
                dve.wait_ge(sg_ready.sem, sg_ready.at(b, e + 1))
                if e >= 2:
                    dve.wait_ge(fy_mm.sem, fy_mm.at(b, e - 1))
                V.tensor_tensor(gg[e % 2][:, :], sg[e % 2][:, :], R[(e + 1) % 2][:, BT:2 * BT], ALU.mult
                                ).then_inc(gg_ready.sem, 1)

            def ffn_add(e, b):
                dve.wait_ge(fy_mm.sem, fy_mm.at(b, e + 1))
                if e == 0:
                    V.tensor_tensor(rb[:, :, :], two(R[2][:, 0:U * DIM]), h4[:, :, :], ALU.add
                                    ).then_inc(fy_taken.sem, 1)
                else:
                    dve.wait_ge(fy_taken.sem, fy_taken.at(b, e))
                    for u in range(U):
                        ins = V.scalar_tensor_tensor(out=rb[:, u, :], in0=R[2][:, u * DIM:(u + 1) * DIM],
                                                     scalar=cw2[:, u, e - 1:e], in1=rb[:, u, :],
                                                     op0=ALU.mult, op1=ALU.add)
                    ins.then_inc(fy_taken.sem, 1)

            def back_end(b):
                dve.wait_ge(fy_taken.sem, fy_taken.at(b, FFN))
                dve.wait_ge(fin_free.sem, fin_free.at(b, 16))
                norm(b, cb, rb, fin, 2, var_b, rstd_b, bb, fin_ready)
                cb.end()

            def step(a, m, b):
                if m is not None:
                    split_h2(m)
                    gate(m)
                if b is not None:
                    scan_part(0, b)
                if a is not None:
                    tok(a)
                if m is not None:
                    gate_bias(m)
                if b is not None:
                    scan_part(1, b)
                if a is not None:
                    qk_l1(a)
                    spread_keys(0, a)
                if m is not None:
                    add_expert(0, m)
                if b is not None:
                    scan_part(2, b)
                if a is not None:
                    linear_mask(a)
                if m is not None:
                    add_expert(1, m)
                if b is not None:
                    scan_part(3, b)
                if a is not None:
                    after_linear(a)
                if m is not None:
                    add_expert(2, m)
                if b is not None:
                    scan_part(4, b)
                if m is not None:
                    add_expert(3, m)
                if a is not None:
                    spread_keys(1, a)
                if b is not None:
                    scan_part(5, b)
                if a is not None:
                    softmax_in(a)
                if m is not None:
                    add_expert(4, m)
                if a is not None:
                    softmax_out(a)
                if b is not None:
                    scan_part(6, b)
                if m is not None:
                    add_expert(5, m)
                if b is not None:
                    scan_part(7, b)
                if m is not None:
                    add_expert(6, m)
                if b is not None:
                    after_scan(b)
                if m is not None:
                    add_expert(7, m)
                    after_experts(m)
                if a is not None:
                    after_softmax(a)
                if b is not None:
                    gate1(b)
                if m is not None:
                    conv(m)
                if b is not None:
                    ffn_mul(0, b)
                    ffn_mul(1, b)
                    ffn_add(0, b)
                    ffn_mul(2, b)
                    ffn_add(1, b)
                    ffn_mul(3, b)
                    ffn_add(2, b)
                if m is not None:
                    bc_split(m)
                if b is not None:
                    ffn_mul(4, b)
                    ffn_add(3, b)
                    ffn_mul(5, b)
                    ffn_add(4, b)
                if m is not None:
                    bc_parts(m)
                if b is not None:
                    ffn_mul(6, b)
                    ffn_add(5, b)
                    ffn_mul(7, b)
                    ffn_add(6, b)
                    ffn_mul(8, b)
                    ffn_add(7, b)
                    ffn_add(8, b)
                    back_end(b)
                if m is not None:
                    softplus(m)

            step(0, None, None)
            step(1, 0, None)
            with dve.Fori(1, BLOCKS - 1) as i:
                step(i + 1, i, i - 1)
            step(None, BLOCKS - 1, BLOCKS - 2)
            step(None, None, BLOCKS - 1)

        @block.gpsimd
        def _(pool):
            G = nc.gpsimd
            pool.wait_ge(ready.sem, 1)
            pool.wait_ge(ld["rows"].sem, 64)
            pool.wait_ge(ld["cst"].sem, 32)

            def power(var, rs, src, dst, k, i):
                pool.wait_ge(var.sem, var.at(i, k))
                G.tensor_tensor(dst[:, :], src[:, :], half_neg[:, :], ALU.pow).then_inc(rs.sem, 1)

            def power_a(k, a):
                power(var_a, rstd_a, ve, rstd, k, a)

            def power_m(m):
                power(var_m, rstd_m, vem, rstdm, 1, m)

            def power_b(k, b):
                power(var_b, rstd_b, veb, rstdb, k, b)

            def add_bias(src, sig, k, row, dst, done, i):
                pool.wait_ge(sig.sem, sig.at(i, k))
                G.tensor_tensor(dst[:, :, :], src[:, :, :], row.unsqueeze(1).broadcast_to([P, U, DIM]), ALU.add
                                ).then_inc(done.sem, 1)

            def rest_w1(e, m):
                for mp in range(HM // 2):
                    unit = e * HM // 2 + mp
                    pool.wait_ge(w1_rounded.sem, w1_rounded.at(m, unit + 1))
                    G.tensor_tensor(w1_lo[unit % RING][:, :, :], w1_raw[:, :, 2 * mp * P:2 * (mp + 1) * P],
                                    w1_hi[unit % RING][:, :, :].bitcast(F32), ALU.subtract
                                    ).then_inc(w1_ready.sem, 1)

            def keep_residual(b):
                pool.wait_ge(h3_ready.sem, h3_ready.at(b, 1))
                G.tensor_tensor(rb[:, :, :], h3[:, :, :], ones[:, 0:1].unsqueeze(2).broadcast_to([P, U, DIM]),
                                ALU.mult).then_inc(kept.sem, 1)

            def sum_residuals(i):
                if not first(i):
                    pool.wait_ge(h3_ready.sem, h3_ready.at(i, 0))
                pool.wait_ge(xm_ready.sem, xm_ready.at(i, 1))
                G.tensor_tensor(acc[:, :, :], h1[:, :, :], xm[:, :, :], ALU.add).then_inc(hx_ready.sem, 1)

            def step_times_u(i):
                pool.wait_ge(delta_ready.sem, delta_ready.at(i, 1))
                pool.wait_ge(u_ready.sem, u_ready.at(i, 1))
                G.tensor_tensor(du[:, :, :], delta[:, :, :], uu[:, :, :], ALU.mult).then_inc(du_ready.sem, 1)

            def add_states(first_step, steps, b):
                for n in range(first_step, first_step + steps):
                    c = n % CH
                    pool.wait_ge(hc_ready.sem, hc_ready.at(b, n + 1))
                    one, two_ = hs[n % SLOTS][:, 0:BT], hs[n % SLOTS][:, BT:2 * BT]
                    if n >= CH:
                        pool.wait_ge(y_added.sem, y_added.at(b, n - CH + 1))
                        G.tensor_tensor(one, one, two_, ALU.add).then_inc(pair_added.sem, 1)
                        pool.wait_ge(pair_added.sem, pair_added.at(b, n - CH + 1))
                        G.tensor_tensor(yy[:, c, :], yy[:, c, :], one, ALU.add).then_inc(y_added.sem, 1)
                    else:
                        G.tensor_tensor(yy[:, c, :], one, two_, ALU.add).then_inc(y_added.sem, 1)

            def gate_y(c, b):
                pool.wait_ge(y_added.sem, y_added.at(b, STEPS - CH + c + 1))
                pool.wait_ge(z_ready.sem, z_ready.at(b, 1))
                G.tensor_tensor(yy[:, c, :], yy[:, c, :], sz[:, c, :], ALU.mult).then_inc(yz_ready.sem, 1)

            def step(a, m, b):
                if m is not None:
                    sum_residuals(m)
                    rest_w1(1, m)
                if a is not None:
                    power_a(1, a)
                    add_bias(h0, h_a, 1, proj1_b, hb, h0b_ready, a)
                if b is not None:
                    add_states(0, 1, b)
                if m is not None:
                    rest_w1(2, m)
                if b is not None:
                    add_states(1, 2, b)
                    keep_residual(b)
                    add_states(3, 1, b)
                if m is not None:
                    rest_w1(3, m)
                if b is not None:
                    add_states(4, 2, b)
                    add_states(6, 1, b)
                if m is not None:
                    rest_w1(4, m)
                if b is not None:
                    add_states(7, 2, b)
                if a is not None:
                    power_a(2, a)
                    power_a(3, a)
                    add_bias(h1, h1_ready, 1, proj2_b, hb, h1b_ready, a)
                if b is not None:
                    add_states(9, 1, b)
                if m is not None:
                    rest_w1(5, m)
                if b is not None:
                    add_states(10, 2, b)
                    add_states(12, 1, b)
                if m is not None:
                    rest_w1(6, m)
                if b is not None:
                    add_states(13, 2, b)
                    add_states(15, 1, b)
                if m is not None:
                    rest_w1(7, m)
                if b is not None:
                    add_states(16, 2, b)
                    add_states(18, 4, b)
                    gate_y(0, b)
                    add_states(22, 1, b)
                    gate_y(1, b)
                    add_states(23, 1, b)
                    gate_y(2, b)
                    power_b(1, b)
                if m is not None:
                    power_m(m)
                if a is not None:
                    power_a(4, a)
                    rest_w1(0, a)
                if b is not None:
                    power_b(2, b)
                if m is not None:
                    step_times_u(m)

            step(0, None, None)
            step(1, 0, None)
            with pool.Fori(1, BLOCKS - 1) as i:
                step(i + 1, i, i - 1)
            step(None, BLOCKS - 1, BLOCKS - 2)
            step(None, None, BLOCKS - 1)

def laid_out(x, weights):
    import numpy as np

    def halves(w):
        return w.reshape(2, HALF, -1).transpose(1, 0, 2)

    def chunks(w, k):
        return w.reshape(k, P, -1).transpose(1, 0, 2)

    w = weights
    own = [(c, r, q) for c in range(CHANNELS) for r in range(PATCH) for q in range(PATCH)]
    ring = [(c, r, q) for c in range(CHANNELS) for r in (-1, PATCH) for q in range(PATCH)]
    ring += [(c, r, q) for c in range(CHANNELS) for r in range(PATCH) for q in (-1, PATCH)]
    pc, pr, pq = np.array(own + ring).T
    padded = np.pad(x, ((0, 0), (0, 0), (1, 1), (1, 1)))
    g = SIDE // PATCH
    ty, tx = np.divmod(np.arange(g * g), g)
    px = padded[:, pc[:, None], pr[:, None] + 1 + PATCH * ty, pq[:, None] + 1 + PATCH * tx]
    px = px.reshape(BLOCKS, BI, PK, PR, SEQ).transpose(0, 3, 2, 1, 4).reshape(BLOCKS, PR, PK * BT)
    rows = np.full((SHIFTS, PIXELS), PATCH_DIM)
    for s, (dr, dq) in enumerate(((0, 0), (0, 1), (0, -1), (1, 0), (-1, 0))):
        r, q = pr + dr, pq + dq
        ok = (r >= 0) & (r < PATCH) & (q >= 0) & (q < PATCH)
        rows[s, ok] = ((r * PATCH + q) * 5 * CHANNELS + s * CHANNELS + pc)[ok]
    at = rows.reshape(SHIFTS, PK, PR).transpose(2, 0, 1)

    def patch(v):
        return np.pad(v, ((0, 1),) + ((0, 0),) * (v.ndim - 1))[at]

    cst = np.zeros((P, C_END), np.float32)
    p = np.arange(P)[:, None]
    cst[:, C_IDENT:C_IDENT + P] = np.eye(P)
    same = (p % 32) // SEQ == np.arange(32) // SEQ
    cst[:, C_MASK:C_MASK + 32] = same
    cst[:, C_NEG:C_NEG + 32] = np.where(same, 0.0, -FAR)
    cst[:, C_HEAD:C_HEAD + HH] = p // HD == np.arange(HH)
    cst[:, C_TRI:C_TRI + 64] = (np.arange(8) < np.arange(8)[:, None]).reshape(1, 64)
    cst[0:PR, C_CNT:C_CNT + PK] = (at < PATCH_DIM).sum(1)
    cols = np.concatenate([w["L1_attn_conv_w"].reshape(INNER, TAPS), w["L1_attn_conv_b"][:, None],
                           w["L1_attn_b_dt"][:, None], w["L1_attn_A_log"]], 1)
    ln1_gb = np.concatenate([w["L0_ffn_" + n].reshape(2, HALF).T for n in ("ln1_g", "ln1_b")], 1)

    def stacks(v):
        return np.stack([v[:P], np.concatenate([v[P:], v[P:]])], 1)

    def stacked(routed, shared):
        return np.concatenate([shared[None], routed])

    f1, f3, f2 = (stacked(w["L1_ffn_w" + n], w["L1_ffn_sw" + n]) for n in "132")
    return {
        "x": px, "cst": cst,
        "tokgb": np.stack([patch(w["L0_tok_ln_gamma"]), patch(w["L0_tok_ln_beta"])], 1),
        "tok_w": patch(w["L0_tok_w"]),
        "rows": np.concatenate([w["L0_tok_b"], w["L0_attn_b_proj"], w["L0_ffn_proj_b"], w["L0_ffn_gate_b"],
                                w["L1_ffn_gate_bias"]]),
        "ln1_gb": ln1_gb,
        "ln2_gb": np.concatenate([stacks(w["L0_ffn_" + n]) for n in ("ln2_g", "ln2_b")], 1), "cols": chunks(cols, CH),
        "qkv1": halves(w["L0_attn_w_qkv"].T), "proj1": halves(w["L0_attn_w_proj"].T),
        "qkv2": halves(w["L0_ffn_qkv_w"]), "proj2": halves(w["L0_ffn_proj_w"]),
        "gate0": stacks(w["L0_ffn_gate_w"]), "b2": w["L0_ffn_b2"],
        "b1": w["L0_ffn_b1"].reshape(EXPERTS * HM, P).T,
        "w1": np.stack([stacks(v) for v in w["L0_ffn_w1"]]),
        "w2": w["L0_ffn_w2"].reshape(EXPERTS, HM, P, DIM).transpose(0, 2, 1, 3),
        "in_w": halves(w["L1_attn_W_in"]), "x_w": chunks(w["L1_attn_W_x"], CH),
        "dt_w": chunks(w["L1_attn_W_dt"], CH), "out_w": chunks(w["L1_attn_W_out"], CH),
        "gate1": halves(w["L1_ffn_gate_weight"].T),
        "f1": halves(f1.reshape(FFN * INTER, DIM).T), "f3": halves(f3.reshape(FFN * INTER, DIM).T),
        "f2": f2.transpose(2, 0, 1),
    }

def kernel(**inputs):
    import numpy as np
    import concourse.bacc as bacc
    from concourse.bass_utils import run_bass_kernel_spmd

    nc = bacc.Bacc("TRN2", target_bir_lowering=False, num_devices=1,
                   dynamic_dma_scratch_size=1024)
    host = {k: np.asarray(v) for k, v in inputs.items()}
    arrays, aps = {}, {}
    for name, a in laid_out(host["x"], host).items():
        a = np.ascontiguousarray(a)
        arrays[f"in_{name}"] = a
        aps[name] = nc.dram_tensor(f"in_{name}", a.shape, mybir.dt.from_np(a.dtype), kind="ExternalInput").ap()
    out = nc.dram_tensor("out", (BLOCKS, U, P, DIM), F32, kind="ExternalOutput").ap()
    tower(nc, aps, out)
    r = run_bass_kernel_spmd(nc, [arrays], core_ids=[0])
    return r.results[0]["out"].reshape(IMAGES, SEQ, DIM)
```
